# Optimizing a Trainium2 kernel written in Bass

```python
import numpy as np
import jax
import jax.numpy as jnp

def _softmax(x, axis=-1):
    return jax.nn.softmax(x, axis=axis)

def _gelu(x):
    return jax.nn.gelu(x, approximate=True)

def _silu(x):
    return jax.nn.silu(x)

def _sigmoid(x):
    return jax.nn.sigmoid(x)

def _layernorm(x, axis=-1, eps=1e-05):
    m = jnp.mean(x, axis=axis, keepdims=True)
    v = jnp.var(x, axis=axis, keepdims=True)
    return (x - m) / jnp.sqrt(v + eps)

def _scatter_add(tgt, idx, src, axis=0):
    return tgt.at[idx].add(src)

def _segment_sum(src, seg, n):
    return jax.ops.segment_sum(src, seg, n)
kernel_name = 'mk_early_fusion_embed_d1_tok_img4096_r4_28623c'

def setup_inputs(seed: int=0):
    np.random.seed(seed)
    _w = jnp.asarray

    def _rec_inputs():
        import jax
        import jax.numpy as jnp
        _rk = jax.random.key(seed)
        x = -0.00348982 + 0.707501 * jax.random.normal(jax.random.fold_in(_rk, 1), (8, 128, 64, 2), jnp.float32)
        x_txt = jax.random.randint(jax.random.fold_in(_rk, 51), (8, 512), 0, 64, jnp.int32)
        return (x, x_txt)
    x, x_txt = _rec_inputs()

    def _L0_tok_setup():
        import jax, jax.numpy as jnp
        import numpy as np
        H, N, S, CH, LEN = (128, 64, 128, 1, 1024)

        def _s4d_kernel(log_dt, C, B, inv_A_real, A_imag, L):
            dt = jnp.exp(log_dt)
            Cc = C[..., 0] + 1j * C[..., 1]
            Bc = B[..., 0] + 1j * B[..., 1]
            A = -jnp.exp(inv_A_real) + 1j * A_imag
            rep = H // A.shape[0]
            A = jnp.tile(A, (rep, 1))
            Bc = jnp.tile(Bc, (rep, 1))
            dtA = A * dt[:, None]
            Cc = Bc[None, :, :] * Cc
            Cc = Cc * (jnp.exp(dtA) - 1.0) / A
            ell = jnp.arange(L, dtype=jnp.float32)
            V = jnp.exp(dtA[:, :, None] * ell)
            K = 2.0 * jnp.einsum('chn,hnl->chl', Cc, V).real
            return K.astype(jnp.float32)
        key = jax.random.key(seed)
        k1, k2 = jax.random.split(key, 2)
        log_dt = jax.random.uniform(k1, (H,), minval=float(np.log(0.001)), maxval=float(np.log(0.1))).astype(jnp.float32)
        inv_A_real = jnp.full((S, N), float(np.log(0.5)), dtype=jnp.float32)
        A_imag = jnp.tile((np.pi * jnp.arange(N, dtype=jnp.float32))[None, :], (S, 1))
        B = jnp.stack([jnp.ones((S, N), jnp.float32), jnp.zeros((S, N), jnp.float32)], axis=-1)
        C = (jax.random.normal(k2, (CH, H, N, 2)) * 0.5 ** 0.5).astype(jnp.float32)
        return {'log_dt': log_dt, 'C': C, 'B': B, 'inv_A_real': inv_A_real, 'A_imag': A_imag, 'L': LEN}
    _L0_tok_all = _L0_tok_setup()
    _L0_tok_in = {k: v for k, v in _L0_tok_all.items() if k in ('log_dt', 'B', 'inv_A_real', 'A_imag')}
    del _L0_tok_all

    def _L0_txt_setup():
        import jax, jax.numpy as jnp
        import numpy as np
        VOCAB = 64
        HDC_DIM = 1024
        DECAY = 0.95
        B, T = (8, 512)

        def _encode_trigrams(char_codebook, idx):
            chars = char_codebook[idx]
            chars_m1 = jnp.roll(chars, 1, axis=1).at[:, 0, :].set(0.0)
            chars_m2 = jnp.roll(chars, 2, axis=1).at[:, :2, :].set(0.0)
            trigrams = chars * jnp.roll(chars_m1, 1, axis=-1) * jnp.roll(chars_m2, 2, axis=-1)
            return 0.7 * trigrams + 0.3 * chars

        def _decay_matrix(T, dtype):
            i = jnp.arange(T)
            diffs = (i[:, None] - i[None, :]).astype(dtype)
            m = jnp.where(diffs >= 0, jnp.asarray(DECAY, dtype) ** diffs, 0.0)
            return m / jnp.sum(m, axis=-1, keepdims=True)
        key = jax.random.key(seed)
        k_cb, k_idx = jax.random.split(key)
        cb = jnp.sign(jax.random.normal(k_cb, (VOCAB, HDC_DIM), dtype=jnp.float32))
        cb = jnp.where(cb == 0, 1.0, cb)
        idx = jax.random.randint(k_idx, (B, T), 0, VOCAB)
        return {'char_codebook': cb, 'idx': idx}
    _L0_txt_all = _L0_txt_setup()
    _L0_txt_in = {k: v for k, v in _L0_txt_all.items() if k in ('char_codebook',)}
    del _L0_txt_all

    def _L0_attn_setup():
        import jax, jax.numpy as jnp
        import numpy as np
        BLOCK_H = 32
        BLOCK_W = 32
        N_FEAT = 1024
        K_FEAT = 1024
        key = jax.random.key(seed)
        k1, k2, k3 = jax.random.split(key, 3)
        data = jax.random.normal(k1, (4, 256, K_FEAT), dtype=jnp.float32)
        weight = jax.random.normal(k2, (N_FEAT, K_FEAT), dtype=jnp.float32) * 0.02
        nb, kb = (N_FEAT // BLOCK_H, K_FEAT // BLOCK_W)
        block_pattern = jax.random.randint(k3, (nb, kb), 0, 2, dtype=jnp.int32)
        mask = jnp.repeat(jnp.repeat(block_pattern, BLOCK_H, axis=0), BLOCK_W, axis=1)
        return {'data': data, 'weight': weight, 'mask': mask}
    _L0_attn_all = _L0_attn_setup()
    _L0_attn_in = {k: v for k, v in _L0_attn_all.items() if k in ('weight', 'mask')}
    del _L0_attn_all

    def _L0_ffn_setup():
        import jax, jax.numpy as jnp
        import numpy as np
        B, S = (4, 512)
        IN, OUT = (1024, 1024)
        SPARSITY = 0.05
        ALPHA = 1.0

        def _dequant(base_packed, scales):
            low = base_packed & 15
            high = base_packed >> 4 & 15
            offs = jnp.stack([low, high], axis=-1).reshape(base_packed.shape[0], -1)
            return (offs.astype(jnp.float32) - 8.0) * scales
        key = jax.random.key(seed)
        k1, k2, k3, k4, k5 = jax.random.split(key, 5)
        x = jax.random.normal(k1, (B, S, IN), dtype=jnp.float32)
        base_packed = jax.random.randint(k2, (OUT, IN // 2), 0, 64, dtype=jnp.int32)
        scales = jax.random.uniform(k3, (OUT, 1), dtype=jnp.float32, minval=0.001, maxval=0.02)
        mask = jax.random.bernoulli(k4, SPARSITY, (OUT, IN))
        w_ortho = jax.random.normal(k5, (OUT, IN), dtype=jnp.float32) * 0.01 * mask
        return {'x': x, 'base_packed': base_packed, 'scales': scales, 'w_ortho': w_ortho}
    _L0_ffn_all = _L0_ffn_setup()
    _L0_ffn_in = {k: v for k, v in _L0_ffn_all.items() if k in ('base_packed', 'scales', 'w_ortho')}
    del _L0_ffn_all
    return {'x': x, 'x_txt': x_txt, 'L0_tok_log_dt': _L0_tok_in['log_dt'], 'L0_tok_B': _L0_tok_in['B'], 'L0_tok_inv_A_real': _L0_tok_in['inv_A_real'], 'L0_tok_A_imag': _L0_tok_in['A_imag'], 'L0_txt_char_codebook': _L0_txt_in['char_codebook'], 'L0_attn_weight': _L0_attn_in['weight'], 'L0_attn_mask': _L0_attn_in['mask'], 'L0_ffn_base_packed': _L0_ffn_in['base_packed'], 'L0_ffn_scales': _L0_ffn_in['scales'], 'L0_ffn_w_ortho': _L0_ffn_in['w_ortho']}

def reference(x, x_txt, L0_tok_log_dt, L0_tok_B, L0_tok_inv_A_real, L0_tok_A_imag, L0_txt_char_codebook, L0_attn_weight, L0_attn_mask, L0_ffn_base_packed, L0_ffn_scales, L0_ffn_w_ortho):
    import jax
    import jax.numpy as jnp

    def _L0_tok_ref(log_dt, C, B, inv_A_real, A_imag, L):
        import jax, jax.numpy as jnp
        import numpy as np
        H, N, S, CH, LEN = (128, 64, 128, 1, 1024)

        def _s4d_kernel(log_dt, C, B, inv_A_real, A_imag, L):
            dt = jnp.exp(log_dt)
            Cc = C[..., 0] + 1j * C[..., 1]
            Bc = B[..., 0] + 1j * B[..., 1]
            A = -jnp.exp(inv_A_real) + 1j * A_imag
            rep = H // A.shape[0]
            A = jnp.tile(A, (rep, 1))
            Bc = jnp.tile(Bc, (rep, 1))
            dtA = A * dt[:, None]
            Cc = Bc[None, :, :] * Cc
            Cc = Cc * (jnp.exp(dtA) - 1.0) / A
            ell = jnp.arange(L, dtype=jnp.float32)
            V = jnp.exp(dtA[:, :, None] * ell)
            K = 2.0 * jnp.einsum('chn,hnl->chl', Cc, V).real
            return K.astype(jnp.float32)
        return _s4d_kernel(log_dt, C, B, inv_A_real, A_imag, L)

    def _L0_txt_ref(char_codebook, idx):
        import jax, jax.numpy as jnp
        import numpy as np
        VOCAB = 64
        HDC_DIM = 1024
        DECAY = 0.95
        B, T = (8, 512)

        def _encode_trigrams(char_codebook, idx):
            chars = char_codebook[idx]
            chars_m1 = jnp.roll(chars, 1, axis=1).at[:, 0, :].set(0.0)
            chars_m2 = jnp.roll(chars, 2, axis=1).at[:, :2, :].set(0.0)
            trigrams = chars * jnp.roll(chars_m1, 1, axis=-1) * jnp.roll(chars_m2, 2, axis=-1)
            return 0.7 * trigrams + 0.3 * chars

        def _decay_matrix(T, dtype):
            i = jnp.arange(T)
            diffs = (i[:, None] - i[None, :]).astype(dtype)
            m = jnp.where(diffs >= 0, jnp.asarray(DECAY, dtype) ** diffs, 0.0)
            return m / jnp.sum(m, axis=-1, keepdims=True)
        hdc = _encode_trigrams(char_codebook, idx)
        M = _decay_matrix(hdc.shape[1], hdc.dtype)
        return jnp.einsum('ts,bsd->btd', M, hdc)

    def _L0_attn_ref(data, weight, mask):
        import jax, jax.numpy as jnp
        import numpy as np
        BLOCK_H = 32
        BLOCK_W = 32
        N_FEAT = 1024
        K_FEAT = 1024
        N, K = weight.shape
        nb, kb = (N // BLOCK_H, K // BLOCK_W)
        block_mask = mask.reshape(nb, BLOCK_H, kb, BLOCK_W).astype(jnp.float32).sum(axis=(1, 3)) > 0
        elem_mask = jnp.repeat(jnp.repeat(block_mask, BLOCK_H, axis=0), BLOCK_W, axis=1)
        w_masked = weight * elem_mask.astype(weight.dtype)
        out = jnp.einsum('bsk,nk->bsn', data, w_masked)
        return out

    def _L0_ffn_ref(x, base_packed, scales, w_ortho):
        import jax, jax.numpy as jnp
        import numpy as np
        B, S = (4, 512)
        IN, OUT = (1024, 1024)
        SPARSITY = 0.05
        ALPHA = 1.0

        def _dequant(base_packed, scales):
            low = base_packed & 15
            high = base_packed >> 4 & 15
            offs = jnp.stack([low, high], axis=-1).reshape(base_packed.shape[0], -1)
            return (offs.astype(jnp.float32) - 8.0) * scales
        w = _dequant(base_packed, scales) + ALPHA * w_ortho
        return jnp.einsum('bsi,oi->bso', x, w)
    h = _L0_tok_ref(L0_tok_log_dt, x, L0_tok_B, L0_tok_inv_A_real, L0_tok_A_imag, 1024)
    h = jnp.concatenate([h, _L0_txt_ref(L0_txt_char_codebook, x_txt)], axis=1)
    h = h + _L0_attn_ref(_layernorm(h, axis=-1), L0_attn_weight, L0_attn_mask)
    h = h + _L0_ffn_ref(_layernorm(h, axis=-1), L0_ffn_base_packed, L0_ffn_scales, L0_ffn_w_ortho)
    return h

_drawn_inputs = setup_inputs


def setup_inputs(seed=0):
    import zlib

    import numpy as np

    out = dict(_drawn_inputs(seed))
    spreads = {'L0_tok_inv_A_real': (-0.6931471824645996, 0.2)}
    factors = {}
    for name, (base, spread) in spreads.items():
        noise = np.random.default_rng([zlib.crc32(name.encode()), seed]).standard_normal(out[name].shape)
        drawn = base * np.exp(spread * noise) if base else spread * noise
        out[name] = jnp.asarray(drawn.astype(out[name].dtype))
    for name, factor in factors.items():
        out[name] = (out[name] * factor).astype(out[name].dtype)
    return out
```

```python
from contextlib import ExitStack

import concourse.bass as bass
from concourse import mybir

ALU = mybir.AluOpType
ACT = mybir.ActivationFunctionType
AX = mybir.AxisListType
F32 = mybir.dt.float32
F16 = mybir.dt.float16
I32 = mybir.dt.int32

P = 128
EPS = 1e-5
DECAY = 0.95
TOP = float(2 ** 15)
ZS = 1024.0
EXPONENT = 0x7F800000
MAGIC = 12582912.0
LOG2E = 1.4426950408889634
LN2_HI, LN2_LO = 0.693359375, -2.12194440e-4
INV_2PI = 0.15915494309189535
PI2_A = 6.28125
PI2_B = round((6.283185307179586 - PI2_A) * 2 ** 21) / 2 ** 21
PI2_C = 6.283185307179586 - PI2_A - PI2_B
PI_DOWN = 3.1415925
RSQRT = 1597463007.0
EXP_POLY = [1 / 5040, 1 / 720, 1 / 120, 1 / 24, 1 / 6, 0.5, 1.0, 1.0]


def fusion_kernel(nc, x, x_txt, log_dt, B, inv_A_real, A_imag, codebook, weight, mask,
                  packed, scales, ortho, out):
    CH, H, N, _ = x.shape
    NB, T = x_txt.shape
    V, D = codebook.shape
    KT = D // P
    HD = D // 2
    TILES = T // P
    CW = 2 * P
    H2 = H // 2
    HG = 8
    GROUPS = H2 // HG
    LOGS = 10
    CONSTS = 12
    LA = 7
    assert D == 1024 and V == 64 and 2 * V == P and N == 64 and H == P
    assert TILES == 4 and CH % 4 == 0 and GROUPS == NB == 8

    with ExitStack() as ctx:
        def sb(name, shape, dt):
            return ctx.enter_context(nc.sbuf_tensor(name, shape, dt))

        def ps(name, shape, dt):
            return ctx.enter_context(nc.psum_tensor(name, shape, dt))

        def sem(name):
            return ctx.enter_context(nc.semaphore(name))

        w1 = [sb(f"w1_{n}", [P, KT, D], F16) for n in ("hi", "lo")]
        w2 = [sb(f"w2_{n}", [P, KT, D], F16) for n in ("hi", "lo")]
        s32 = [sb(f"s32_{n}", [P, KT, CW], F32) for n in range(2)]
        s_hi = [sb(f"s_hi{n}", [P, KT, CW], F16) for n in range(2)]
        s_lo = [sb(f"s_lo{n}", [P, KT, CW], F16) for n in range(2)]
        tok = sb("tok", [P, KT, CH, H], F32)
        hrow = [sb(f"hrow{n}", [P, D], F32) for n in range(TILES)]
        z = sb("z", [P, D], F32)
        z_hi = sb("z_hi", [P, KT, P], F16)
        z_lo = sb("z_lo", [P, KT, P], F16)
        ident = sb("ident", [P, P], F32)
        ones = sb("ones", [P, P], F32)
        blocks = sb("blocks", [P, P], F32)
        decay = sb("decay", [P, CW], F32)
        cb = sb("cb", [P, D + 2], F16)
        pid = sb("pid", [P, 1], I32)
        pidf = sb("pidf", [P, 1], F32)
        idx = [sb("idx0", [P, CW], I32), sb("idx1", [P, CW + 2], I32)]
        hot = [sb(f"hot{n}", [P, CW + 2], F16) for n in range(2)]
        c1s = sb("c1s", [P, CW], F32)
        prod = sb("prod", [P, CW], F32)
        enc = sb("enc", [P, CW], F32)
        cs = sb("cs", [P, 16], F32)
        ws = [sb(f"ws{n}", [P, 8], F32) for n in range(2)]
        one_max = sb("one_max", [1, 4], F32)
        rowscale = sb("rowscale", [P, TILES + 1], F32)
        rowcoef = sb("rowcoef", [P, TILES + 1], F32)
        sums = sb("sums", [P, KT], F32)
        nmean = sb("nmean", [P, KT], F32)
        squares = sb("squares", [P, 2, KT], F32)
        mred = sb("mred", [P, 2, 32], F32)
        bmask = sb("bmask", [P, 2, 32], F32)
        sc8 = sb("sc8", [P, 2, KT], F32)
        kmax = sb("kmax", [P, GROUPS], F32)
        ks = sb("ks", [P, 4], F32)
        eps = sb("eps", [P, 1], F32)
        norm = sb("norm", [P, H2], F32)
        bn = [sb(f"bn{n}", [P, 2, 6], F32) for n in range(2)]
        mv = [sb(f"mv{n}", [P, 2], F32) for n in range(2)]
        ln = [sb(f"ln{n}", [P, 8], F32) for n in range(2)]
        U = sb("U", [P, HG, 2, P], F32)
        Ut = sb("Ut", [P, HG, 2, P // 2], F32)
        Y = sb("Y", [P, HG, 2, KT, CH], F32)
        Yb = sb("Yb", [P, HG, 2, 2, KT * CH], F32)
        C = sb("C", [P, CH, 2, H2], F32)
        ein = sb("ein", [P, 2, H2], F32)
        prm = sb("prm", [P, 3, H2], F32)
        zg = sb("zg", [P, 2, LOGS, HG], F32)
        zp = sb("zp", [P, 2, LOGS, H2], F32)

        psT = ps("psT", [P, 2, HD], F32)
        psA = ps("psA", [P, 2, HD], F32)
        psB = ps("psB", [P, 2, HD], F32)
        psG = ps("psG", [P, 2, HD], F32)

        w1_nat = tok[:, :, :, :].rearrange("p a b c -> p a (b c)")

        def w2_nat(r):
            return hrow[2 + r][:, :] if r < 2 else w1_nat[:, r - 2, :]

        cb_nat = hrow[0]
        junk = Y[:, :, :, :, :].rearrange("p a b c d -> p (a b c d)")
        sig = z
        w2hi_i = w2[0][:, :, :].rearrange("p a b -> p (a b)").bitcast(I32)
        w2lo_i = w2[1][:, :, :].rearrange("p a b -> p (a b)").bitcast(I32)
        w2hi_f = w2[0][:, :, :].rearrange("p a b -> p (a b)").bitcast(F32)
        w2lo_f = w2[1][:, :, :].rearrange("p a b -> p (a b)").bitcast(F32)
        MB = 3
        mk = [s32[1][:, :, :].rearrange("p a b -> p (a b)").bitcast(I32)[:, 0:D],
              s32[1][:, :, :].rearrange("p a b -> p (a b)").bitcast(I32)[:, D:2 * D],
              w2[1][:, 0:2, :].rearrange("p a b -> p (a b)").bitcast(I32)]
        tok_heads = tok[:, :, :, :].rearrange("p b c (a h) -> p (b c) a h", a=2)
        x_nat = U[0:H2, :, :, :].rearrange("p a b c -> p (a b c)")
        ai_nat = Yb[0:H2, 0, :, :, :].rearrange("p a b c -> p (a b c)")
        b_nat = Yb[0:H2, 1, :, :, :].rearrange("p a b c -> p (a b c)")
        NT = LOGS * H2
        uf = U[:, :, :, :].rearrange("p a b c -> p (a b c)")
        yf = Yb[:, :, :, :, :].rearrange("p a b c d -> p (a b c d)")
        tmp = [uf[:, n * NT:(n + 1) * NT] for n in range(3)] + [yf[:, n * NT:(n + 1) * NT] for n in range(3)]

        ld_cb, ld_pk, ld_sc, ld_tok, ld_x = (sem(n) for n in ("ld_cb", "ld_pk", "ld_sc", "ld_tok", "ld_x"))
        ld_w = [sem(f"ld_w{r}") for r in range(KT)]
        ld_mk = [sem(f"ld_mk{n}") for n in range(MB)]
        ld_or = [sem(f"ld_or{r}") for r in range(KT)]
        ld_idx = [sem("ld_idx0"), sem("ld_idx1")]
        stored = [sem(f"stored{n}") for n in range(TILES)]
        consts = sem("consts")
        dstep = sem("dstep")
        col_ready, row_laid, top_ready, top_spread = (
            sem(n) for n in ("col_ready", "row_laid", "top_ready", "top_spread"))
        sig_ready, sig_turned, sig_read = sem("sig_ready"), sem("sig_turned"), sem("sig_read")
        cb_scaled, cb_hi, cb_ready = sem("cb_scaled"), sem("cb_hi"), sem("cb_ready")
        tok_turned, tok_taken = sem("tok_turned"), sem("tok_taken")
        mask_summed, mask_spread, mask_read = sem("mask_summed"), sem("mask_spread"), sem("mask_read")
        masked, mean_ready, w1_squared, centred = (
            sem(n) for n in ("masked", "mean_ready", "w1_squared", "centred"))
        nibbles, dequant, w2_built, w2_squared = (
            sem(n) for n in ("nibbles", "dequant", "w2_built", "w2_squared"))
        w_scaled = [sem("w1_scaled"), sem("w2_scaled")]
        w_turned = [sem("w1_turned"), sem("w2_turned")]
        w_hi = [sem("w1_hi_ready"), sem("w2_hi_ready")]
        w_lo = [sem("w1_lo_ready"), sem("w2_lo_ready")]
        hot_ready, c12_done, c0_done = sem("hot_ready"), sem("c12_done"), sem("c0_done")
        c1_ready, prod_ready, enc_ready, scanned = (
            sem(n) for n in ("c1_ready", "prod_ready", "enc_ready", "scanned"))
        hi_ready, lo_ready, tok_copied = sem("hi_ready"), sem("lo_ready"), sem("tok_copied")
        th_done, hrow_ready, l1_done, h1_ready = (
            sem(n) for n in ("th_done", "hrow_ready", "l1_done", "h1_ready"))
        t2_done, zhi_ready, zlo_ready, l2_done, out_ready = (
            sem(n) for n in ("t2_done", "zhi_ready", "zlo_ready", "l2_done", "out_ready"))
        z_ready = sem("z_ready")
        ln_step = [sem("ln1_step"), sem("ln2_step")]
        std_ready = [sem("std1_ready"), sem("std2_ready")]
        LNS, LN_VAR, LN_OUT = 8, 3, 8
        pool_step = sem("pool_step")
        base_ready, norm_ready, sines = sem("base_ready"), sem("norm_ready"), sem("sines")
        uy_ready, kmm_done, tok_ready, kmax_ready, tok_scaled = (
            sem(n) for n in ("uy_ready", "kmm_done", "tok_ready", "kmax_ready", "tok_scaled"))

        def after(eng, s, count):
            if not isinstance(count, int) or count > 0:
                eng.wait_ge(s, count)

        NBT = NB + CH // TILES

        def text_batch(g):
            return not isinstance(g, int) or g < NB

        def makes(g, j):
            if not isinstance(g, int):
                return "text"
            q = 2 * g + j // 2 + 1
            return "text" if q < 2 * NB else "token" if q < 2 * NBT else None

        def group_of(g, j):
            if isinstance(g, int) and g >= NB - 1:
                return NB - 1 if (g, j) == (NB - 1, 1) else None
            return g if j == 3 else None

        def whole(eng, tile):
            for j in range(TILES):
                tile(0, j)
            with eng.Fori(1, NB - 1) as g:
                for j in range(TILES):
                    tile(g, j)
            for g in range(NB - 1, NBT):
                for j in range(TILES):
                    tile(g, j)

        def turn_bank(m):
            return (psT if m % 4 < 2 else psB)[:, m % 2, :]

        block = ctx.enter_context(nc.Block())

        @block.sync
        def _(sp):
            def load_idx(g, par):
                if isinstance(g, int):
                    row = x_txt[g:g + 1, 0:CW] if par == 0 else x_txt[g:g + 1, CW - 2:T]
                else:
                    row = x_txt[bass.ds(g, 1), 0:CW] if par == 0 else x_txt[bass.ds(g, 1), CW - 2:T]
                sp.dma_start(idx[par][:, :], row.broadcast_to([P, row.shape[1]])).then_inc(ld_idx[par], 16)

            for half in range(2):
                sp.dma_start(cb_nat[half * V:(half + 1) * V, :], codebook).then_inc(ld_cb, 16)
            load_idx(0, 0)
            load_idx(0, 1)
            for hh in range(2):
                sp.dma_start(ai_nat[:, hh * N:(hh + 1) * N], inv_A_real[hh * H2:(hh + 1) * H2, :]).then_inc(ld_tok, 16)
                sp.dma_start(ai_nat[:, P + hh * N:P + (hh + 1) * N],
                             A_imag[hh * H2:(hh + 1) * H2, :]).then_inc(ld_tok, 16)
                sp.dma_start(b_nat[:, hh * P:(hh + 1) * P],
                             B[hh * H2:(hh + 1) * H2, :, :].rearrange("h n r -> h (n r)")).then_inc(ld_tok, 16)
                sp.dma_start(ein[hh * N:(hh + 1) * N, 0, :],
                             log_dt[hh * H2:(hh + 1) * H2].rearrange("(a h) -> a h", a=1).broadcast_to([N, H2]))\
                    .then_inc(ld_tok, 16)
                sp.dma_start(x_nat.rearrange("p (c q) -> p c q", c=CH)[:, :, hh * P:(hh + 1) * P],
                             x[:, hh * H2:(hh + 1) * H2, :, :].rearrange("c h n r -> h c (n r)"))\
                    .then_inc(ld_x, 16)
            sp.dma_start(sc8[:, 0, :], scales.rearrange("(r p) a -> p (r a)", p=P),
                         allow_slow_non_contiguous=True).then_inc(ld_sc, 16)
            for r in range(KT):
                after(sp, mask_summed, r - MB + 1)
                sp.dma_start(mk[r % MB], mask[r * P:(r + 1) * P, :]).then_inc(ld_mk[r % MB], 16)
                sp.dma_start(w1_nat[:, r, :], weight[r * P:(r + 1) * P, :]).then_inc(ld_w[r], 16)
            sp.wait_ge(mask_summed, KT)
            sp.dma_start(w2hi_i.rearrange("p (r k) -> p r k", r=KT), packed.rearrange("(r p) k -> p r k", p=P)).then_inc(ld_pk, 16)
            for r in range(KT):
                if r == 2:
                    sp.wait_ge(w_turned[0], 2 * KT)
                sp.dma_start(w2_nat(r), ortho[r * P:(r + 1) * P, :]).then_inc(ld_or[r], 16)

            def text_out(g, j):
                rows = slice(H + j * P, H + (j + 1) * P)
                return out[g, rows, :] if isinstance(g, int) else \
                    out[bass.ds(g, 1), rows, :].rearrange("a p d -> (a p) d")

            def store(g, j):
                i = TILES * g + j
                sp.wait_ge(out_ready, 2 * i + 2)
                dst = out[TILES * (g - NB) + j, 0:H, :] if isinstance(g, int) and g >= NB else text_out(g, j)
                sp.dma_start(dst, hrow[j][:, :]).then_inc(stored[j], 16)

            def tile(g, j):
                if j % 2 == 0 and (not isinstance(g, int) or g < NB - 1):
                    sp.wait_ge(hot_ready, 2 * g + j // 2 + 1)
                    load_idx(g + 1, j // 2)
                if j >= 2:
                    store(g, j - 2)
                elif not isinstance(g, int) or g > 0:
                    store(g - 1, j + 2)

            whole(sp, tile)
            store(NBT - 1, 2)
            store(NBT - 1, 3)
            for j in range(TILES):
                sp.wait_ge(stored[j], 16 * (NBT))

        @block.tensor
        def _(pe):
            def spread_max(n, col):
                pe.wait_ge(col_ready, n)
                pe.matmul(psA[0:1, 0, 0:P], col, ident[:, :], start=True, stop=True).then_inc(row_laid, 1)
                pe.wait_ge(top_ready, n)
                pe.matmul(psA[:, 1, 0:1], ones[0:1, :], one_max[0:1, 0:1], start=True, stop=True)\
                    .then_inc(top_spread, 1)

            def gather(q, d, par):
                n = KT * q + d
                if d == 0:
                    pe.wait_ge(hot_ready, q + 1)
                after(pe, prod_ready, n)
                pe.matmul(psG[:, 0, 0:CW], cb[:, 1 + d * P:1 + (d + 1) * P], hot[par][:, 1:CW + 1],
                          start=True, stop=True)
                pe.matmul(psG[:, 0, CW:2 * CW], cb[:, d * P:(d + 1) * P], hot[par][:, 0:CW],
                          start=True, stop=True).then_inc(c12_done, 1)
                after(pe, enc_ready, n)
                pe.matmul(psG[:, 1, 0:CW], cb[:, 2 + d * P:2 + (d + 1) * P], hot[par][:, 2:CW + 2],
                          start=True, stop=True).then_inc(c0_done, 1)

            def rows_form(q, j, text):
                off = (j % 2) * P
                for d in range(KT):
                    if j % 2 == 0:
                        if text:
                            pe.wait_ge(scanned, KT * q + d + 1)
                        else:
                            pe.wait_ge(tok_copied, KT * (q - 2 * NB) + d + 1)
                    mm = pe.transpose(psT[:, d // 4, (d % 4) * P:(d % 4 + 1) * P],
                                      s32[j // 2][:, d, off:off + P], ident[:, :])
                    if d % 4 == 3:
                        mm.then_inc(th_done, 1)

            def layer1(q, i, j, h):
                off = (j % 2) * P
                after(pe, h1_ready, 2 * (i - 1) + h + 1)
                for k in range(KT):
                    if j % 2 == 0 and h == 0:
                        pe.wait_ge(hi_ready, KT * q + k + 1)
                        pe.wait_ge(lo_ready, KT * q + k + 1)
                    hi, lo = s_hi[j // 2][:, k, off:off + P], s_lo[j // 2][:, k, off:off + P]
                    wh, wl = (w[:, k, h * HD:(h + 1) * HD] for w in w1)
                    pe.matmul(psA[:, h, :], hi, wh, start=(k == 0), stop=False)
                    pe.matmul(psA[:, h, :], hi, wl, start=False, stop=False)
                    mm = pe.matmul(psA[:, h, :], lo, wh, start=False, stop=(k == KT - 1))
                mm.then_inc(l1_done, 1)

            def turn_z(i, follows):
                pe.wait_ge(z_ready, i + 1)
                for d in range(KT):
                    if d % 4 == 0 and follows:
                        pe.wait_ge(hrow_ready, 2 * i + 2 + d // 4 + 1)
                    mm = pe.transpose(psT[:, d // 4, (d % 4) * P:(d % 4 + 1) * P],
                                      z[:, d * P:(d + 1) * P], ident[:, :])
                    if d % 4 == 3:
                        mm.then_inc(t2_done, 1)

            def layer2(i, h):
                after(pe, out_ready, 2 * (i - 1) + h + 1)
                for k in range(KT):
                    if h == 0 and k % 4 == 0:
                        pe.wait_ge(zlo_ready, 2 * i + k // 4 + 1)
                    wh, wl = (w[:, k, h * HD:(h + 1) * HD] for w in w2)
                    pe.matmul(psB[:, h, :], z_hi[:, k, :], wh, start=(k == 0), stop=False)
                    pe.matmul(psB[:, h, :], z_hi[:, k, :], wl, start=False, stop=False)
                    mm = pe.matmul(psB[:, h, :], z_lo[:, k, :], wh, start=False, stop=(k == KT - 1))
                mm.then_inc(l2_done, 1)

            def token_group(g):
                pe.wait_ge(uy_ready, g + 1)
                for u in range(HG):
                    for ri in range(2):
                        mm = pe.matmul(psT[:, u // 4, (u % 4) * P:(u % 4 + 1) * P], U[:, u, ri, :],
                                       Yb[:, u, ri, :, :].rearrange("p a b -> p (a b)"),
                                       start=(ri == 0), stop=(ri == 1))
                    if u % 4 == 3:
                        mm.then_inc(kmm_done, 1)

            def turn_weights(l, nat):
                for m in range(2 * KT):
                    k, half = m // 2, m % 2
                    after(pe, w_lo[l], m - 3)
                    for u in range(4):
                        mm = pe.transpose(turn_bank(m)[:, u * P:(u + 1) * P],
                                          nat(half * 4 + u)[:, k * P:(k + 1) * P], ident[:, :])
                    mm.then_inc(w_turned[l], 1)
                pe.wait_ge(w_lo[l], 2 * KT)

            pe.wait_ge(consts, CONSTS)
            spread_max(1, cs[:, 0:1])
            pe.wait_ge(sig_ready, 1)
            for j in range(TILES):
                mm = pe.transpose(psB[:, 0, j * P:(j + 1) * P], sig[:, HD + j * P:HD + (j + 1) * P],
                                  ident[:, :])
            mm.then_inc(sig_turned, 1)
            pe.wait_ge(ld_tok, 16 * 8)
            pe.wait_ge(ld_x, 32)
            small = ident[0:H2, 0:H2]
            for n in range(2):
                pe.transpose(psT[:, 0, n * H2:(n + 1) * H2], ai_nat[:, n * P:(n + 1) * P], small)
            for n in range(2):
                mm = pe.transpose(psT[:, 0, (2 + n) * H2:(3 + n) * H2],
                                  b_nat[:, 0:2 * P].rearrange("p (m r) -> p m r", r=2)[:, :, n], small)
            mm.then_inc(tok_turned, 1)
            for half in range(2):
                for m in range(CH):
                    c, ri = half * (CH // 2) + m // 2, m % 2
                    src = x_nat.rearrange("p (c m r) -> p c m r", c=CH, r=2)[:, c, :, ri]
                    mm = pe.transpose((psT if half == 0 else psB)[:, 1, m * H2:(m + 1) * H2], src, small)
                mm.then_inc(tok_turned, 1)
            pe.wait_ge(cb_ready, 2)
            for r in range(KT):
                gather(0, r, 0)
                pe.wait_ge(mask_summed, r + 1)
                if r < 2:
                    pe.wait_ge(tok_taken, 2)
                after(pe, mask_read, r - 1)
                pe.matmul(psT[:, r % 2, 0:32], blocks[:, :], mred[:, r % 2, :], start=True, stop=True)\
                    .then_inc(mask_spread, 1)
            spread_max(2, ws[0][:, 0:1])
            pe.wait_ge(centred, KT)
            pe.wait_ge(mask_read, KT)
            pe.wait_ge(tok_taken, 3)
            pe.wait_ge(sig_read, 1)
            turn_weights(0, lambda r: w1_nat[:, r, :])

            def tile(g, j):
                i, q, kind = TILES * g + j, 2 * g + j // 2, makes(g, j)
                second = not (isinstance(g, int) and g == 0 and j == 0)

                def slot(s):
                    if kind == "text":
                        gather(q + 1, 4 * (j % 2) + s, (j // 2 + 1) % 2)

                rows_form(q, j, text_batch(g))
                slot(0)
                layer1(q, i, j, 0)
                if second:
                    turn_z(i - 1, True)
                slot(1)
                layer1(q, i, j, 1)
                if isinstance(g, int) and g == 0 and j == 1:
                    pe.wait_ge(h1_ready, 2 * i + 2)
                    spread_max(3, ws[1][:, 0:1])
                    pe.wait_ge(zlo_ready, 2)
                    turn_weights(1, w2_nat)
                slot(2)
                if second:
                    layer2(i - 1, 0)
                group = group_of(g, j)
                if group is not None:
                    token_group(group)
                slot(3)
                if second:
                    layer2(i - 1, 1)
                if group is not None:
                    pe.wait_ge(tok_ready, 2 * group + 2)
                if isinstance(g, int) and (g, j) == (NB - 1, 1):
                    pe.wait_ge(h1_ready, 2 * i + 2)
                    spread_max(4, ks[:, 0:1])
                    pe.wait_ge(tok_scaled, 1)

            whole(pe, tile)
            last = TILES * NBT - 1
            turn_z(last, False)
            layer2(last, 0)
            layer2(last, 1)

        @block.scalar
        def _(act):
            def gathered(n):
                act.wait_ge(c12_done, n + 1)
                after(act, prod_ready, n)
                act.activation(c1s[:, :], psG[:, 0, 0:CW], ACT.Identity, scale=cs[:, 8:9]).then_inc(c1_ready, 1)

            def high(n, par, d, made, m):
                act.wait_ge(made, m + 1)
                act.activation(s_hi[par][:, d, :], s32[par][:, d, :], ACT.Copy).then_inc(hi_ready, 1)

            def weights_high(l, w):
                act.wait_ge(w_scaled[l], 1)
                for m in range(2 * KT):
                    k, half = m // 2, m % 2
                    act.wait_ge(w_turned[l], m + 1)
                    act.activation(w[0][:, k, half * HD:(half + 1) * HD], turn_bank(m), ACT.Identity,
                                   scale=ws[l][:, 1:2]).then_inc(w_hi[l], 1)

            act.wait_ge(cb_scaled, 1)
            act.activation(cb[:, 2:D + 2], cb_nat[:, :], ACT.Identity, scale=cs[:, 3:4]).then_inc(cb_hi, 1)
            act.activation(cb[:, 0:2], cb_nat[:, D - 2:D], ACT.Identity, scale=cs[:, 3:4]).then_inc(cb_hi, 1)
            act.wait_ge(tok_turned, 1)
            act.activation(ein[:, 1, :], psT[:, 0, 0:H2], ACT.Copy)
            act.activation(prm[:, :, :].rearrange("p a b -> p (a b)"), psT[:, 0, H2:4 * H2], ACT.Copy)\
                .then_inc(tok_taken, 1)
            for half in range(2):
                act.wait_ge(tok_turned, 2 + half)
                act.activation(C[:, half * 4:(half + 1) * 4, :, :].rearrange("p a b c -> p (a b c)"),
                               (psT if half == 0 else psB)[:, 1, :], ACT.Copy).then_inc(tok_taken, 1)
            for r in range(KT):
                gathered(r)
                high(r, 0, r, scanned, r)
                act.wait_ge(masked, r + 1)
                act.activation(junk, w1_nat[:, r, :], ACT.Square, accum_out=squares[:, 0, r:r + 1])\
                    .then_inc(w1_squared, 1)
                act.wait_ge(mean_ready, r + 1)
                act.wait_ge(w1_squared, r + 1)
                act.activation(w1_nat[:, r, :], w1_nat[:, r, :], ACT.Identity, bias=nmean[:, r:r + 1])\
                    .then_inc(centred, 1)
            weights_high(0, w1)

            def tile(g, j):
                i, q, kind = TILES * g + j, 2 * g + j // 2, makes(g, j)
                text, par = text_batch(g), (j // 2 + 1) % 2
                col = j if text else TILES

                def slot_in(s):
                    d = 4 * (j % 2) + s
                    if kind == "text":
                        gathered(KT * (q + 1) + d)
                    elif kind == "token":
                        c = 2 * (q + 1 - 2 * NB)
                        act.wait_ge(tok_scaled, 1)
                        act.wait_ge(l1_done, 2 * i)
                        act.activation(s32[par][:, d, :], tok[:, d, c:c + 2, :].rearrange("p a b -> p (a b)"),
                                       ACT.Identity, scale=ks[:, 1:2]).then_inc(tok_copied, 1)

                def slot_out(s):
                    d = 4 * (j % 2) + s
                    if kind == "text":
                        high(KT * (q + 1) + d, par, d, scanned, KT * (q + 1) + d)
                    elif kind == "token":
                        high(KT * (q + 1) + d, par, d, tok_copied, KT * (q + 1 - 2 * NB) + d)

                def std(l):
                    act.wait_ge(ln_step[l], LNS * i + LN_VAR)
                    act.activation(ln[l][:, 5:6], mv[l][:, 1:2], ACT.Sqrt, bias=eps[:, :])\
                        .then_inc(std_ready[l], 1)

                for h in range(2):
                    act.wait_ge(th_done, 2 * i + h + 1)
                    if h == 0:
                        after(act, stored[j], 16 * g)
                    act.activation(hrow[j][:, h * HD:(h + 1) * HD], psT[:, h, :], ACT.Identity,
                                   scale=rowscale[:, col:col + 1]).then_inc(hrow_ready, 1)
                slot_in(0)
                std(0)
                slot_out(0)
                if not (isinstance(g, int) and g == 0 and j == 0):
                    z_high(i - 1)
                slot_in(1)
                slot_out(1)
                if isinstance(g, int) and g == 0 and j == 1:
                    for r in range(KT):
                        act.wait_ge(w2_built, r + 1)
                        after(act, w2_squared, r)
                        act.activation(junk, w2_nat(r), ACT.Square, accum_out=squares[:, 1, r:r + 1])\
                            .then_inc(w2_squared, 1)
                    weights_high(1, w2)
                slot_in(2)
                std(1)
                slot_out(2)
                act.wait_ge(ln_step[1], LNS * i + LN_OUT)
                after(act, t2_done, 2 * i)
                act.activation(z[:, :], hrow[j][:, :], ACT.Identity, bias=ln[1][:, 4:5],
                               scale=ln[1][:, 3:4]).then_inc(z_ready, 1)
                slot_in(3)
                slot_out(3)
                group = group_of(g, j)
                if group is not None:
                    for b in range(2):
                        act.wait_ge(kmm_done, 2 * group + b + 1)
                        first = HG * group + 4 * b
                        act.activation(
                            tok_heads[:, :, :, bass.ds(first, 4)].rearrange("p m a u -> p u a m"),
                            psT[:, b, :].rearrange("p (u a m) -> p u a m", u=4, a=2), ACT.Copy)\
                            .then_inc(tok_ready, 1)
                if isinstance(g, int) and g == 0 and j == 0:
                    act.wait_ge(nibbles, 3)
                    for r in range(KT):
                        for f, n in ((w2lo_f, w2lo_i), (w2hi_f, w2hi_i)):
                            act.activation(f[:, r * HD:(r + 1) * HD], n[:, r * HD:(r + 1) * HD], ACT.Identity,
                                           bias=sc8[:, 1, r:r + 1], scale=sc8[:, 0, r:r + 1])\
                                .then_inc(dequant, 1)
                    act.wait_ge(base_ready, 1)
                    act.activation(tmp[3], tmp[0], ACT.Sin)
                    act.activation(tmp[4], tmp[0], ACT.Sin, scale=0.5).then_inc(sines, 1)

            def z_high(i):
                for b in range(2):
                    act.wait_ge(t2_done, 2 * i + b + 1)
                    if b == 0:
                        after(act, l2_done, 2 * i)
                    act.activation(z_hi[:, 4 * b:4 * b + 4, :].rearrange("p a b -> p (a b)"), psT[:, b, :],
                                   ACT.Copy, scale=ZS).then_inc(zhi_ready, 1)

            whole(act, tile)
            z_high(TILES * NBT - 1)

        @block.vector
        def _(dve):
            steps = [0]

            def link(ins):
                steps[0] += 1
                ins.then_inc(dstep, 1)
                dve.wait_ge(dstep, steps[0])

            def power_of_two(out, in_):
                link(dve.tensor_scalar(out.bitcast(I32), in_.bitcast(I32), EXPONENT, None, ALU.bitwise_and))

            def spread_max(n):
                dve.wait_ge(row_laid, n)
                dve.tensor_reduce(one_max[0:1, 0:1], psA[0:1, 0, 0:P], AX.X, ALU.max).then_inc(top_ready, 1)
                dve.wait_ge(top_spread, n)

            def weight_scale(l):
                w = ws[l]
                spread_max(2 + l)
                link(dve.tensor_scalar(w[:, 3:4], psA[:, 1, 0:1], 1e-30, None, ALU.max))
                link(dve.tensor_scalar(w[:, 4:5].bitcast(I32), w[:, 3:4].bitcast(I32), 1, None,
                                       ALU.logical_shift_right))
                link(dve.tensor_scalar(w[:, 5:6].bitcast(I32), w[:, 4:5].bitcast(I32), -1.0, RSQRT,
                                       ALU.mult, ALU.add))
                link(dve.tensor_scalar(w[:, 6:7], w[:, 5:6], TOP / 2, None, ALU.mult))
                power_of_two(w[:, 1:2], w[:, 6:7])
                link(dve.reciprocal(w[:, 2:3], w[:, 1:2]))
                if l == 1:
                    link(dve.tensor_scalar(w[:, 7:8], w[:, 2:3], 1.0 / ZS, None, ALU.mult))

            def weights_low(l, w):
                for m in range(2 * KT):
                    k, half = m // 2, m % 2
                    dve.wait_ge(w_hi[l], m + 1)
                    part = slice(half * HD, (half + 1) * HD)
                    dve.scalar_tensor_tensor(out=w[1][:, k, part], in0=turn_bank(m), scalar=ws[l][:, 1:2],
                                             in1=w[0][:, k, part], op0=ALU.mult, op1=ALU.subtract)\
                        .then_inc(w_lo[l], 1)

            def one_hot(q, par):
                cols = CW if par == 0 else CW + 2
                loaded = 16 * (q // 2 + 1) if isinstance(q, int) else 16 * batch_of[0]
                dve.wait_ge(ld_idx[par], loaded)
                after(dve, c0_done, KT * (q - 1))
                dve.tensor_scalar(hot[par][:, CW + 2 - cols:CW + 2], idx[par][:, :], pidf[:, 0:1], None,
                                  ALU.is_equal).then_inc(hot_ready, 1)

            batch_of = [None]

            def encode(q, d, par, i):
                n = KT * q + d
                dve.wait_ge(c1_ready, n + 1)
                dve.tensor_tensor(prod[:, :], c1s[:, :], psG[:, 0, CW:2 * CW], ALU.mult).then_inc(prod_ready, 1)
                dve.wait_ge(prod_ready, n + 1)
                dve.wait_ge(c0_done, n + 1)
                dve.scalar_tensor_tensor(out=enc[:, :], in0=prod[:, :], scalar=cs[:, 9:10], in1=psG[:, 1, 0:CW],
                                         op0=ALU.add, op1=ALU.mult).then_inc(enc_ready, 1)
                dve.wait_ge(enc_ready, n + 1)
                if i is not None and d % 4 == 0:
                    after(dve, l1_done, 2 * i)
                if par == 1:
                    dve.wait_ge(scanned, n - KT + 1)
                dve.tensor_tensor_scan(s32[par][:, d, :], decay[:, :], enc[:, :],
                                       0.0 if par == 0 else s32[0][:, d, CW - 1:CW],
                                       ALU.mult, ALU.add).then_inc(scanned, 1)

            def low(n, par, d):
                dve.wait_ge(hi_ready, n + 1)
                dve.tensor_tensor(s_lo[par][:, d, :], s32[par][:, d, :], s_hi[par][:, d, :], ALU.subtract)\
                    .then_inc(lo_ready, 1)

            dve.wait_ge(ld_cb, 32)
            dve.tensor_reduce(cs[:, 0:1], cb_nat[:, :], AX.X, ALU.max, apply_absolute_value=True)\
                .then_inc(col_ready, 1)
            dve.wait_ge(consts, CONSTS)
            link(dve.tensor_tensor_scan(sig[:, HD:HD + CW], decay[:, :], sig[:, 0:CW], 0.0, ALU.mult, ALU.add))
            dve.tensor_tensor_scan(sig[:, HD + CW:D], decay[:, :], sig[:, CW:HD], sig[:, HD + CW - 1:HD + CW],
                                   ALU.mult, ALU.add).then_inc(sig_ready, 1)
            dve.wait_ge(consts, CONSTS)
            for par in range(2):
                link(dve.memset(hot[par][:, 0:2], 0.0))
            one_hot(0, 0)
            spread_max(1)
            link(dve.tensor_scalar(cs[:, 1:2], psA[:, 1, 0:1], 1e-30, None, ALU.max))
            link(dve.reciprocal(cs[:, 2:3], cs[:, 1:2]))
            link(dve.tensor_scalar(cs[:, 4:5], cs[:, 2:3], TOP, None, ALU.mult))
            power_of_two(cs[:, 3:4], cs[:, 4:5])
            link(dve.reciprocal(cs[:, 5:6], cs[:, 3:4]))
            cb_scale_steps = steps[0]
            link(dve.tensor_scalar(cs[:, 6:7], cs[:, 1:2], cs[:, 1:2], 0.7, ALU.mult, ALU.mult))
            link(dve.tensor_scalar(cs[:, 6:7], cs[:, 6:7], 0.3, cs[:, 1:2], ALU.add, ALU.mult))
            link(dve.reciprocal(cs[:, 7:8], cs[:, 6:7]))
            link(dve.tensor_scalar(cs[:, 7:8], cs[:, 7:8], TOP * (1 - DECAY), None, ALU.mult))
            power_of_two(cs[:, 7:8], cs[:, 7:8])
            link(dve.tensor_tensor(cs[:, 10:11], cs[:, 7:8], cs[:, 5:6], ALU.mult))
            link(dve.tensor_scalar(cs[:, 9:10], cs[:, 10:11], 0.3, None, ALU.mult))
            link(dve.tensor_scalar(cs[:, 11:12], cs[:, 10:11], cs[:, 5:6], 0.7, ALU.mult, ALU.mult))
            dve.tensor_tensor(cs[:, 8:9], cs[:, 11:12], cs[:, 5:6], ALU.mult).then_inc(cb_scaled, 1)
            for n, (to, of) in enumerate(((slice(2, D + 2), slice(0, D)), (slice(0, 2), slice(D - 2, D)))):
                dve.wait_ge(cb_hi, n + 1)
                dve.scalar_tensor_tensor(out=cb[V:P, to], in0=cb_nat[V:P, of], scalar=cs[V:P, 3:4],
                                         in1=cb[V:P, to], op0=ALU.mult, op1=ALU.subtract).then_inc(cb_ready, 1)
            dve.wait_ge(sig_turned, 1)
            link(dve.tensor_scalar(rowscale[:, 0:TILES], psB[:, 0, :].rearrange("p (j t) -> p j t", j=TILES)[:, :, 0],
                                   cs[:, 7:8], None, ALU.mult))
            dve.reciprocal(rowscale[:, 0:TILES], rowscale[:, 0:TILES]).then_inc(sig_read, 1)

            for r in range(KT):
                dve.wait_ge(ld_mk[r % MB], 16 * (r // MB + 1))
                after(dve, mask_spread, r - 1)
                dve.tensor_reduce(mred[:, r % 2, :], mk[r % MB].rearrange("p (b w) -> p b w", w=32), AX.X,
                                  ALU.add).then_inc(mask_summed, 1)
                encode(0, r, 0, None)
                dve.wait_ge(mask_spread, r + 1)
                after(dve, masked, r - 1)
                dve.tensor_scalar(bmask[:, r % 2, :], psT[:, r % 2, 0:32], 0.0, None, ALU.is_gt)\
                    .then_inc(mask_read, 1)
                dve.wait_ge(mask_read, r + 1)
                dve.wait_ge(ld_w[r], 16)
                wr = w1_nat[:, r, :].rearrange("p (b w) -> p b w", w=32)
                dve.scalar_tensor_tensor(out=wr, in0=wr, scalar=1.0,
                                         in1=bmask[:, r % 2, :].unsqueeze(2).to_broadcast([P, 32, 32]),
                                         op0=ALU.mult, op1=ALU.mult, accum_out=sums[:, r:r + 1])\
                    .then_inc(masked, 1)
                dve.wait_ge(masked, r + 1)
                dve.tensor_scalar(nmean[:, r:r + 1], sums[:, r:r + 1], -1.0 / D, None, ALU.mult)\
                    .then_inc(mean_ready, 1)
                low(r, 0, r)
            dve.wait_ge(w1_squared, KT)
            dve.tensor_reduce(ws[0][:, 0:1], squares[:, 0, :], AX.X, ALU.max).then_inc(col_ready, 1)
            weight_scale(0)
            dve.wait_ge(sig_read, 1)
            dve.tensor_scalar(rowcoef[:, 0:TILES], rowscale[:, 0:TILES], ws[0][:, 2:3], None, ALU.mult)\
                .then_inc(w_scaled[0], 1)
            dve.wait_ge(ld_sc, 16)
            dve.tensor_scalar(sc8[:, 1, :], sc8[:, 0, :], -8.0, None, ALU.mult).then_inc(nibbles, 1)
            dve.wait_ge(ld_pk, 16)
            dve.tensor_scalar(w2lo_i, w2hi_i, 15, None, ALU.bitwise_and).then_inc(nibbles, 1)
            dve.wait_ge(nibbles, 2)
            dve.tensor_scalar(w2hi_i, w2hi_i, 4, 15, ALU.logical_shift_right, ALU.bitwise_and).then_inc(nibbles, 1)
            weights_low(0, w1)

            def normalise(l, i, scale_col):
                w, s, base = ln[l], ln_step[l], LNS * i
                dve.wait_ge(std_ready[l], i + 1)
                if l == 1:
                    after(dve, z_ready, i)
                dve.reciprocal(w[:, 1:2], w[:, 5:6]).then_inc(s, 1)
                dve.wait_ge(s, base + 5)
                dve.scalar_tensor_tensor(out=w[:, 2:3], in0=w[:, 1:2], scalar=w[:, 1:2], in1=w[:, 0:1],
                                         op0=ALU.mult, op1=ALU.mult).then_inc(s, 1)
                dve.wait_ge(s, base + 6)
                dve.scalar_tensor_tensor(out=w[:, 3:4], in0=w[:, 2:3], scalar=1.5, in1=w[:, 1:2],
                                         op0=ALU.add, op1=ALU.mult).then_inc(s, 1)
                dve.wait_ge(s, base + 7)
                if l == 0:
                    dve.tensor_tensor(w[:, 4:5], w[:, 3:4], scale_col, ALU.mult).then_inc(s, 1)
                else:
                    dve.scalar_tensor_tensor(out=w[:, 4:5], in0=w[:, 3:4], scalar=-1.0, in1=mv[1][:, 0:1],
                                             op0=ALU.mult, op1=ALU.mult).then_inc(s, 1)

            def statistics(l, i, j, ready):
                s, base = ln_step[l], LNS * i
                for h in range(2):
                    dve.wait_ge(ready, 2 * i + h + 1)
                    dve.bn_stats(bn[l][:, h, :], hrow[j][:, h * HD:(h + 1) * HD]).then_inc(s, 1)
                dve.wait_ge(s, base + 2)
                dve.memset(ln[l][:, 6:7], 0.0)
                dve.bn_aggr(mv[l][:, :], bn[l][:, :, :].rearrange("p a b -> p (a b)")).then_inc(s, 1)
                dve.wait_ge(s, base + 3)
                dve.tensor_scalar(ln[l][:, 0:1], mv[l][:, 1:2], EPS, -0.5, ALU.add, ALU.mult).then_inc(s, 1)

            def finish(i, j, h):
                dve.wait_ge(l2_done, 2 * i + h + 1)
                part = hrow[j][:, h * HD:(h + 1) * HD]
                dve.scalar_tensor_tensor(out=part, in0=psB[:, h, :], scalar=ws[1][:, 7:8], in1=part,
                                         op0=ALU.mult, op1=ALU.add).then_inc(out_ready, 1)

            def z_low(i):
                for b in range(2):
                    dve.wait_ge(zhi_ready, 2 * i + b + 1)
                    part = slice(4 * b, 4 * b + 4)
                    dve.scalar_tensor_tensor(out=z_lo[:, part, :].rearrange("p a b -> p (a b)"), in0=psT[:, b, :],
                                             scalar=ZS, in1=z_hi[:, part, :].rearrange("p a b -> p (a b)"),
                                             op0=ALU.mult, op1=ALU.subtract).then_inc(zlo_ready, 1)

            def tile(g, j):
                i, q, kind = TILES * g + j, 2 * g + j // 2, makes(g, j)
                text, par = text_batch(g), (j // 2 + 1) % 2
                first = isinstance(g, int) and g == 0
                batch_of[0] = g + 1 + j // 2

                def slot_in(s):
                    if kind == "text":
                        encode(q + 1, 4 * (j % 2) + s, par, i)

                def slot_out(s):
                    if kind is not None:
                        low(KT * (q + 1) + 4 * (j % 2) + s, par, 4 * (j % 2) + s)

                def residual(h):
                    dve.wait_ge(l1_done, 2 * i + h + 1)
                    part = hrow[j][:, h * HD:(h + 1) * HD]
                    dve.scalar_tensor_tensor(out=part, in0=psA[:, h, :], scalar=ln[0][:, 4:5], in1=part,
                                             op0=ALU.mult, op1=ALU.add).then_inc(h1_ready, 1)

                if not first or j >= 2:
                    finish(i - 2, (j + 2) % 4, 1)
                if kind == "text" and j % 2 == 0:
                    one_hot(q + 1, par)
                statistics(0, i, j, hrow_ready)
                slot_in(0)
                col = j if text else TILES
                normalise(0, i, rowcoef[:, col:col + 1])
                slot_out(0)
                dve.wait_ge(ln_step[0], LNS * i + LN_OUT)
                residual(0)
                if not first or j >= 1:
                    z_low(i - 1)
                slot_in(1)
                slot_out(1)
                residual(1)
                statistics(1, i, j, h1_ready)
                if first and j == 1:
                    dve.wait_ge(w2_squared, KT)
                    dve.tensor_reduce(ws[1][:, 0:1], squares[:, 1, :], AX.X, ALU.max).then_inc(col_ready, 1)
                    weight_scale(1)
                    dve.tensor_copy(ws[1][:, 3:4], ws[1][:, 2:3]).then_inc(w_scaled[1], 1)
                    weights_low(1, w2)
                slot_in(2)
                normalise(1, i, None)
                slot_out(2)
                if not first or j >= 1:
                    finish(i - 1, (j + 3) % 4, 0)
                slot_in(3)
                slot_out(3)
                group = group_of(g, j)
                if group is not None:
                    dve.wait_ge(tok_ready, 2 * group + 2)
                    dve.tensor_reduce(kmax[:, bass.ds(group, 1)], tok_heads[:, :, :, bass.ds(HG * group, HG)],
                                      AX.XYZ, ALU.max, apply_absolute_value=True).then_inc(kmax_ready, 1)
                if isinstance(g, int) and (g, j) == (NB - 1, 1):
                    dve.wait_ge(kmax_ready, GROUPS)
                    dve.tensor_reduce(ks[:, 0:1], kmax[:, :], AX.X, ALU.max).then_inc(col_ready, 1)
                    spread_max(4)
                    link(dve.tensor_scalar(ks[:, 2:3], psA[:, 1, 0:1], 1e-30, None, ALU.max))
                    link(dve.reciprocal(ks[:, 3:4], ks[:, 2:3]))
                    link(dve.tensor_scalar(ks[:, 3:4], ks[:, 3:4], TOP, None, ALU.mult))
                    power_of_two(ks[:, 1:2], ks[:, 3:4])
                    link(dve.reciprocal(rowscale[:, TILES:TILES + 1], ks[:, 1:2]))
                    dve.tensor_tensor(rowcoef[:, TILES:TILES + 1], rowscale[:, TILES:TILES + 1], ws[0][:, 2:3],
                                      ALU.mult).then_inc(tok_scaled, 1)

            def invert_norm():
                dve.wait_ge(base_ready, 1)
                dve.reciprocal(norm[:, :], norm[:, :]).then_inc(norm_ready, 1)

            dve_tile = tile

            def tile_and_norm(g, j):
                dve_tile(g, j)
                if isinstance(g, int) and (g, j) == (0, 0):
                    invert_norm()

            whole(dve, tile_and_norm)
            last = TILES * NBT - 1
            finish(last - 1, 2, 1)
            z_low(last)
            finish(last, 3, 0)
            finish(last, 3, 1)

        @block.gpsimd
        def _(pool):
            made = [0]

            def const(ins):
                made[0] += 1
                ins.then_inc(consts, 1)
                pool.wait_ge(consts, made[0])

            const(pool.memset(ident[:, :], 0.0))
            const(pool.affine_select(out=ident[:, :], in_=ident[:, :], compare_op=ALU.not_equal, fill=1.0, base=0,
                                     pattern=[[-1, P]], channel_multiplier=1))
            const(pool.memset(decay[:, :], DECAY))
            const(pool.memset(sig[:, 0:HD], 1.0))
            const(pool.memset(ones[:, :], 1.0))
            const(pool.memset(eps[:, :], EPS))
            for half in range(2):
                const(pool.iota(pid[half * V:(half + 1) * V, :], pattern=[[0, 1]], base=0, channel_multiplier=1))
            const(pool.tensor_copy(pidf[:, :], pid[:, :]))
            const(pool.memset(blocks[:, :], 1.0))
            const(pool.affine_select(out=blocks[:, :].rearrange("p (a b) -> p a b", b=32),
                                     in_=blocks[:, :].rearrange("p (a b) -> p a b", b=32), compare_op=ALU.is_ge,
                                     fill=0.0, base=0, pattern=[[-32, 4], [0, 32]], channel_multiplier=1))
            const(pool.affine_select(out=blocks[:, :].rearrange("p (a b) -> p a b", b=32),
                                     in_=blocks[:, :].rearrange("p (a b) -> p a b", b=32), compare_op=ALU.is_ge,
                                     fill=0.0, base=31, pattern=[[32, 4], [0, 32]], channel_multiplier=-1))
            assert made[0] == CONSTS

            count = [0]

            def link(ins):
                count[0] = count[0] + 1
                ins.then_inc(pool_step, 1)
                pool.wait_ge(pool_step, count[0])

            def ts(out, in_, s1, op0, s2=None, op1=ALU.bypass):
                link(pool.tensor_scalar(out, in_, s1, s2, op0, op1) if s2 is not None
                     else pool.tensor_scalar(out, in_, s1, None, op0))

            def tt(out, a, b, op):
                link(pool.tensor_tensor(out, a, b, op))

            def exp(dst, src, k, r, p):
                ts(src, src, 87.0, ALU.min, -87.0, ALU.max)
                ts(k, src, LOG2E, ALU.mult, MAGIC, ALU.add)
                ts(k, k, -MAGIC, ALU.add)
                ts(r, k, -LN2_HI, ALU.mult)
                tt(r, r, src, ALU.add)
                ts(p, k, -LN2_LO, ALU.mult)
                tt(r, r, p, ALU.add)
                ts(p, r, EXP_POLY[0], ALU.mult, EXP_POLY[1], ALU.add)
                for c in EXP_POLY[2:]:
                    tt(p, p, r, ALU.mult)
                    ts(p, p, c, ALU.add)
                ts(k.bitcast(I32), k, 127.0, ALU.add, float(2 ** 23), ALU.mult)
                tt(dst, p, k, ALU.mult)

            pool.wait_ge(tok_taken, 3)
            flat = ein[:, :, :].rearrange("p a b -> p (a b)")
            exp(flat, flat, tmp[0][:, 0:2 * H2], tmp[1][:, 0:2 * H2], tmp[2][:, 0:2 * H2])
            dt_, ea, ai = ein[:, 0, :], ein[:, 1, :], prm[:, 0, :]
            q3 = tmp[0].rearrange("p (j h) -> p j h", j=LOGS)
            x3 = tmp[3].rearrange("p (j h) -> p j h", j=LOGS)
            tt(q3[:, 0, :], ai, dt_, ALU.mult)
            tt(x3[:, 0, :], ea, dt_, ALU.mult)
            ts(x3[:, 0, :], x3[:, 0, :], -1.0, ALU.mult)
            for l in range(1, LOGS):
                ts(q3[:, l, :], q3[:, l - 1, :], 2.0, ALU.mult)
                ts(x3[:, l, :], x3[:, l - 1, :], 2.0, ALU.mult)
            ts(tmp[1], tmp[0], INV_2PI, ALU.mult, MAGIC, ALU.add)
            ts(tmp[1], tmp[1], -MAGIC, ALU.add)
            for part in (PI2_A, PI2_B, PI2_C):
                ts(tmp[2], tmp[1], -part, ALU.mult)
                tt(tmp[0], tmp[0], tmp[2], ALU.add)
            ts(tmp[0], tmp[0], PI_DOWN, ALU.min, -PI_DOWN, ALU.max)
            exp(tmp[5], tmp[3], tmp[1], tmp[2], tmp[4])
            tt(norm[:, :], ea, ea, ALU.mult)
            tt(tmp[1][:, 0:H2], ai, ai, ALU.mult)
            pool.tensor_tensor(norm[:, :], norm[:, :], tmp[1][:, 0:H2], ALU.add).then_inc(base_ready, 1)

            for r in range(KT):
                pool.wait_ge(dequant, 2 * r + 2)
                pool.wait_ge(ld_or[r], 16)
                pair = w2_nat(r).rearrange("p (m b) -> p m b", b=2)
                pool.tensor_tensor(pair[:, :, 0], pair[:, :, 0], w2lo_f[:, r * HD:(r + 1) * HD], ALU.add)
                pool.tensor_tensor(pair[:, :, 1], pair[:, :, 1], w2hi_f[:, r * HD:(r + 1) * HD], ALU.add)\
                    .then_inc(w2_built, 1)

            pool.wait_ge(sines, 1)
            zr, zi = (zp[:, n, :, :].rearrange("p a b -> p (a b)") for n in range(2))
            tt(tmp[4], tmp[4], tmp[4], ALU.mult)
            ts(tmp[4], tmp[4], -2.0, ALU.mult, 1.0, ALU.add)
            tt(zr, tmp[4], tmp[5], ALU.mult)
            tt(zi, tmp[3], tmp[5], ALU.mult)
            br, bi = prm[:, 1, :], prm[:, 2, :]
            er, gr, gi, t0, t1 = (tmp[0][:, n * H2:(n + 1) * H2] for n in range(5))
            fr, fi = (tmp[1][:, n * H2:(n + 1) * H2] for n in range(2))
            ts(er, zp[:, 0, 0, :], -1.0, ALU.add)
            ei = zp[:, 1, 0, :]
            tt(t0, er, ea, ALU.mult)
            tt(t1, ei, ai, ALU.mult)
            tt(fr, t1, t0, ALU.subtract)
            tt(t0, er, ai, ALU.mult)
            tt(t1, ei, ea, ALU.mult)
            tt(fi, t0, t1, ALU.add)
            pool.wait_ge(norm_ready, 1)
            tt(fr, fr, norm[:, :], ALU.mult)
            tt(fi, fi, norm[:, :], ALU.mult)
            ts(fr, fr, 2.0, ALU.mult)
            ts(fi, fi, -2.0, ALU.mult)
            tt(t0, fr, br, ALU.mult)
            tt(t1, fi, bi, ALU.mult)
            tt(gr, t0, t1, ALU.subtract)
            tt(t0, fr, bi, ALU.mult)
            tt(t1, fi, br, ALU.mult)
            tt(gi, t0, t1, ALU.add)
            cr, ci = C[:, :, 0, :], C[:, :, 1, :]
            grb, gib = (v.unsqueeze(1).to_broadcast([P, CH, H2]) for v in (gr, gi))
            a0, a1, a2, a3 = (tmp[n][:, 0:CH * H2].rearrange("p (c h) -> p c h", c=CH) for n in (2, 3, 4, 5))
            tt(a0, cr, grb, ALU.mult)
            tt(a1, ci, gib, ALU.mult)
            tt(a2, cr, gib, ALU.mult)
            tt(a3, ci, grb, ALU.mult)
            tt(cr, a0, a1, ALU.subtract)
            tt(a2, a2, a3, ALU.add)
            ts(ci, a2, -1.0, ALU.mult)
            link(pool.memset(yf, 0.0))
            link(pool.memset(U[:, :, 0, 0:1], 1.0))
            link(pool.memset(U[:, :, 1, 0:1], 0.0))
            pool.wait_ge(w2_squared, KT)

            done = count[0]
            GSTEPS = 4 + 4 * LA + 4 * (LOGS - LA) + 1

            def group(g):
                at = [0]

                def signal(ins):
                    at[0] += 1
                    ins.then_inc(pool_step, 1)

                def step(ins):
                    signal(ins)
                    pool.wait_ge(pool_step, done + GSTEPS * g + at[0])

                after(pool, kmm_done, 2 * g)
                heads = bass.ds(HG * g, HG)
                for ri in range(2):
                    signal(pool.tensor_tensor(zg[:, ri, :, :], zp[:, ri, :, heads],
                                              ones[:, 0:LOGS * HG].rearrange("p (a b) -> p a b", a=LOGS), ALU.mult))
                    signal(pool.tensor_copy(Y[:, :, ri, 0, :].rearrange("p h c -> p c h"), C[:, :, ri, heads]))
                pool.wait_ge(pool_step, done + GSTEPS * g + at[0])

                def double(t, src, dst, scratch, l, w, conj):
                    shape = [P, HG, 2, w]
                    zr_, zi_ = (zg[:, n, l, :].unsqueeze(2).unsqueeze(3).to_broadcast(shape) for n in range(2))
                    step(pool.tensor_tensor(dst, src, zr_, ALU.mult))
                    step(pool.tensor_tensor(scratch, src, zi_, ALU.mult))
                    step(pool.tensor_tensor(dst[:, :, 0, :], dst[:, :, 0, :], scratch[:, :, 1, :],
                                            ALU.add if conj else ALU.subtract))
                    step(pool.tensor_tensor(dst[:, :, 1, :], dst[:, :, 1, :], scratch[:, :, 0, :],
                                            ALU.subtract if conj else ALU.add))

                for l in range(LA):
                    w = 2 ** l
                    double(U, U[:, :, :, 0:w], U[:, :, :, w:2 * w], Ut[:, :, :, 0:w], l, w, False)
                y4 = Y[:, :, :, :, :].rearrange("p h r b c -> p h r (b c)")
                for l in range(LA, LOGS):
                    w = CH * 2 ** (l - LA)
                    double(Y, y4[:, :, :, 0:w], y4[:, :, :, w:2 * w], Ut[:, :, :, 0:w], l, w, True)
                one = ones[0:N, 0:KT * CH].unsqueeze(1).unsqueeze(2).to_broadcast([N, HG, 2, KT * CH])
                signal(pool.tensor_tensor(Yb[0:N, :, :, 0, :], y4[0:N, :, :, :], one, ALU.mult))
                pool.tensor_copy(Yb[N:P, :, :, 1, :], y4[N:P, :, :, :]).then_inc(uy_ready, 1)
                assert at[0] == GSTEPS

            group(0)
            with pool.Fori(1, GROUPS) as g:
                group(g)


_INS = ["x", "x_txt", "L0_tok_log_dt", "L0_tok_B", "L0_tok_inv_A_real", "L0_tok_A_imag", "L0_txt_char_codebook",
        "L0_attn_weight", "L0_attn_mask", "L0_ffn_base_packed", "L0_ffn_scales", "L0_ffn_w_ortho"]


def kernel(**inputs):
    import numpy as _np
    import concourse.bacc as _bacc
    from concourse import mybir as _mybir
    from concourse.bass_utils import run_bass_kernel_spmd as _run

    nc = _bacc.Bacc("TRN2", target_bir_lowering=False, num_devices=1)
    arrays, args = {}, []
    for name in _INS:
        a = _np.ascontiguousarray(inputs[name])
        arrays[f"in_{name}"] = a
        args.append(nc.dram_tensor(f"in_{name}", a.shape, _mybir.dt.from_np(a.dtype), kind="ExternalInput").ap())
    heads, times, features = inputs["x"].shape[1], inputs["x_txt"].shape[1], inputs["L0_attn_weight"].shape[0]
    shape = (inputs["x"].shape[0], heads + times, features)
    args.append(nc.dram_tensor("out", shape, _mybir.dt.float32, kind="ExternalOutput").ap())
    fusion_kernel(nc, *args)
    r = _run(nc, [arrays], core_ids=[0])
    return r.results[0]["out"]
```

```python
from contextlib import ExitStack

import concourse.bass as bass
from concourse import mybir

ALU = mybir.AluOpType
ACT = mybir.ActivationFunctionType
AX = mybir.AxisListType
F32 = mybir.dt.float32
F16 = mybir.dt.float16
I32 = mybir.dt.int32

P = 128
EPS = 1e-5
DECAY = 0.95
TOP = float(2 ** 15)
ZS = 1024.0
EXPONENT = 0x7F800000
MAGIC = 12582912.0
LOG2E = 1.4426950408889634
LN2_HI, LN2_LO = 0.693359375, -2.12194440e-4
INV_2PI = 0.15915494309189535
PI2_A = 6.28125
PI2_B = round((6.283185307179586 - PI2_A) * 2 ** 21) / 2 ** 21
PI2_C = 6.283185307179586 - PI2_A - PI2_B
PI_DOWN = 3.1415925
RSQRT = 1597463007.0 + 14 * 2.0 ** 23
EXP_POLY = [1 / 5040, 1 / 720, 1 / 120, 1 / 24, 1 / 6, 0.5, 1.0, 1.0]


def fusion_kernel(nc, x, x_txt, log_dt, B, inv_A_real, A_imag, codebook, weight, mask,
                  packed, scales, ortho, out):
    CH, H, N, _ = x.shape
    NB, T = x_txt.shape
    V, D = codebook.shape
    KT = D // P
    HD = D // 2
    TILES = T // P
    CW = 2 * P
    H2 = H // 2
    HG = 8
    GROUPS = H2 // HG
    LOGS = 10
    CONSTS = 12
    LA = 7
    assert D == 1024 and V == 64 and 2 * V == P and N == 64 and H == P
    assert TILES == 4 and CH % 4 == 0 and GROUPS == NB == 8

    with ExitStack() as ctx:
        def sb(name, shape, dt):
            return ctx.enter_context(nc.sbuf_tensor(name, shape, dt))

        def ps(name, shape, dt):
            return ctx.enter_context(nc.psum_tensor(name, shape, dt))

        def sem(name):
            return ctx.enter_context(nc.semaphore(name))

        w1 = [sb(f"w1_{n}", [P, KT, D], F16) for n in ("hi", "lo")]
        w2 = [sb(f"w2_{n}", [P, KT, D], F16) for n in ("hi", "lo")]
        s32 = [sb("s32_0", [P, KT, CW], F32), sb("s32_1", [P, 4, CW], F32)]
        s_hi = [sb(f"s_hi{n}", [P, KT, CW], F16) for n in range(2)]
        s_lo = [sb(f"s_lo{n}", [P, KT, CW], F16) for n in range(2)]
        tok = sb("tok", [P, KT, CH, H], F32)
        hrow = [sb(f"hrow{n}", [P, D], F32) for n in range(TILES)]
        h_rows = [sb(f"h_rows_{n}", [P, KT, 2, P], F16) for n in ("hi", "lo")]
        z = sb("z", [P, D], F32)
        z_parts = sb("z_parts", [P, 2, D], F16)
        z_rows = [z_parts[:, n, :] for n in range(2)]
        z_hi = sb("z_hi", [P, KT, P], F16)
        z_lo = sb("z_lo", [P, KT, P], F16)
        ident = sb("ident", [P, P], F32)
        ones = sb("ones", [P, P], F32)
        blocks = sb("blocks", [P, P], F32)
        decay = sb("decay", [P, CW], F32)
        cb = sb("cb", [P, D + 2], F16)
        pid = sb("pid", [P, 1], I32)
        pidf = sb("pidf", [P, 1], F32)
        idx = [sb("idx0", [P, CW], I32), sb("idx1", [P, CW + 2], I32)]
        hot = [sb(f"hot{n}", [P, CW + 2], F16) for n in range(2)]
        c1s = sb("c1s", [P, CW], F32)
        prod = sb("prod", [P, CW], F32)
        cs = sb("cs", [P, 16], F32)
        ws = [sb(f"ws{n}", [P, 8], F32) for n in range(2)]
        one_max = sb("one_max", [1, 4], F32)
        rowscale = sb("rowscale", [P, TILES + 1], F32)
        rowcoef = sb("rowcoef", [P, TILES + 1], F32)
        sums = sb("sums", [P, KT], F32)
        nmean = sb("nmean", [P, KT], F32)
        squares = sb("squares", [P, 2, KT], F32)
        mred = sb("mred", [P, 2, 32], F32)
        bmask = sb("bmask", [P, 2, 32], F32)
        sc = sb("sc", [P, KT], F32)
        sc28 = sb("sc28", [P, KT], F32)
        sq8 = sb("sq8", [P, KT], F32)
        kmax = sb("kmax", [P, GROUPS], F32)
        ks = sb("ks", [P, 4], F32)
        eps = sb("eps", [P, 1], F32)
        norm = sb("norm", [P, H2], F32)
        bn = [sb(f"bn{n}", [P, 2, 6], F32) for n in range(2)]
        mv = [sb(f"mv{n}", [P, 2], F32) for n in range(2)]
        ln = [sb(f"ln{n}", [P, 8], F32) for n in range(2)]
        U = sb("U", [P, HG, 2, P], F32)
        Ut = sb("Ut", [P, HG, 2, P // 2], F32)
        Y = sb("Y", [P, HG, 2, KT, CH], F32)
        Yb = sb("Yb", [P, HG, 2, 2, KT * CH], F32)
        C = sb("C", [P, CH, 2, H2], F32)
        ein = sb("ein", [P, 2, H2], F32)
        prm = sb("prm", [P, 3, H2], F32)
        zg = sb("zg", [P, 2, LOGS, HG], F32)
        zp = sb("zp", [P, 2, LOGS, H2], F32)

        psT = ps("psT", [P, 2, HD], F32)
        psA = ps("psA", [P, 2, HD], F32)
        psB = ps("psB", [P, 2, HD], F32)
        psG = ps("psG", [P, 2, HD], F32)

        w1_nat = tok[:, :, :, :].rearrange("p a b c -> p a (b c)")

        def w2_nat(r):
            return hrow[2 + r][:, :] if r < 2 else w1_nat[:, r - 2, :]

        cb_nat = hrow[0]
        junk = Y[:, :, :, :, :].rearrange("p a b c d -> p (a b c d)")
        sig = z
        w2hi_i = w2[0][:, :, :].rearrange("p a b -> p (a b)").bitcast(I32)
        w2lo_i = w2[1][:, :, :].rearrange("p a b -> p (a b)").bitcast(I32)
        MB = 3
        mk = [s32[1][:, :, :].rearrange("p a b -> p (a b)").bitcast(I32),
              z_parts[:, :, :].rearrange("p a b -> p (a b)").bitcast(I32),
              w2[1][:, 0:2, :].rearrange("p a b -> p (a b)").bitcast(I32)]
        tok_heads = tok[:, :, :, :].rearrange("p b c (a h) -> p (b c) a h", a=2)
        x_nat = U[0:H2, :, :, :].rearrange("p a b c -> p (a b c)")
        ai_nat = Yb[0:H2, 0, :, :, :].rearrange("p a b c -> p (a b c)")
        b_nat = Yb[0:H2, 1, :, :, :].rearrange("p a b c -> p (a b c)")
        z_last = [U[:, 4 * n:4 * n + 4, :, :].rearrange("p a b c -> p (a b c)").bitcast(F16)[:, 0:D]
                  .rearrange("p (a b) -> p a b", a=KT) for n in range(2)]
        NT = LOGS * H2
        uf = U[:, :, :, :].rearrange("p a b c -> p (a b c)")
        yf = Yb[:, :, :, :, :].rearrange("p a b c d -> p (a b c d)")
        tmp = [uf[:, n * NT:(n + 1) * NT] for n in range(3)] + [yf[:, n * NT:(n + 1) * NT] for n in range(3)]

        ld_cb, ld_pk, ld_sc, ld_tok, ld_x = (sem(n) for n in ("ld_cb", "ld_pk", "ld_sc", "ld_tok", "ld_x"))
        ld_w = [sem(f"ld_w{r}") for r in range(KT)]
        ld_mk = [sem(f"ld_mk{n}") for n in range(MB)]
        ld_or = [sem(f"ld_or{r}") for r in range(KT)]
        ld_idx = [sem("ld_idx0"), sem("ld_idx1")]
        stored = [sem(f"stored{n}") for n in range(TILES)]
        consts = sem("consts")
        dstep = sem("dstep")
        col_ready, row_laid, top_ready, top_spread = (
            sem(n) for n in ("col_ready", "row_laid", "top_ready", "top_spread"))
        sig_ready, sig_turned, sig_read = sem("sig_ready"), sem("sig_turned"), sem("sig_read")
        cb_scaled, cb_hi, cb_ready = sem("cb_scaled"), sem("cb_hi"), sem("cb_ready")
        tok_turned, tok_taken = sem("tok_turned"), sem("tok_taken")
        mask_summed, mask_spread, mask_read = sem("mask_summed"), sem("mask_spread"), sem("mask_read")
        masked, mean_ready, w1_squared, centred = (
            sem(n) for n in ("masked", "mean_ready", "w1_squared", "centred"))
        nibbles, w2_built, w2_squared = (sem(n) for n in ("nibbles", "w2_built", "w2_squared"))
        w_scaled = [sem("w1_scaled"), sem("w2_scaled")]
        w_turned = [sem("w1_turned"), sem("w2_turned")]
        w_hi = [sem("w1_hi_ready"), sem("w2_hi_ready")]
        w_lo = [sem("w1_lo_ready"), sem("w2_lo_ready")]
        hot_ready, c12_done, c0_done = sem("hot_ready"), sem("c12_done"), sem("c0_done")
        c1_ready, prod_ready, enc_ready, scanned = (
            sem(n) for n in ("c1_ready", "prod_ready", "enc_ready", "scanned"))
        hi_ready, lo_ready, tok_copied = sem("hi_ready"), sem("lo_ready"), sem("tok_copied")
        l1_done, h1_ready, l2_done, out_ready = (
            sem(n) for n in ("l1_done", "h1_ready", "l2_done", "out_ready"))
        hhi_ready, hrow_ready, z_ready, zhi_ready, zlo_ready = (
            sem(n) for n in ("hhi_ready", "hrow_ready", "z_ready", "zhi_ready", "zlo_ready"))
        h_turned, z_turned = [sem("h_turned0"), sem("h_turned1")], sem("z_turned")
        turn_allowed = sem("turn_allowed")
        ln_step = [sem("ln1_step"), sem("ln2_step")]
        std_ready = [sem("std1_ready"), sem("std2_ready")]
        LNS, LN_VAR, LN_OUT = 8, 3, 8
        pool_step = sem("pool_step")
        base_ready, norm_ready, sines = sem("base_ready"), sem("norm_ready"), sem("sines")
        uy_ready, kmm_done, tok_ready, kmax_ready, tok_scaled = (
            sem(n) for n in ("uy_ready", "kmm_done", "tok_ready", "kmax_ready", "tok_scaled"))

        def after(eng, s, count):
            if not isinstance(count, int) or count > 0:
                eng.wait_ge(s, count)

        NBT = NB + CH // TILES

        def text_batch(g):
            return not isinstance(g, int) or g < NB

        def makes(g, j):
            if not isinstance(g, int):
                return "text"
            q = 2 * g + j // 2 + 1
            return "text" if q < 2 * NB else "token" if q < 2 * NBT else None

        def group_of(g, j):
            if isinstance(g, int) and g >= NB - 1:
                return NB - 1 if (g, j) == (NB - 1, 1) else None
            return g if j == 3 else None

        def whole(eng, tile):
            for j in range(TILES):
                tile(0, j)
            with eng.Fori(1, NB - 1) as g:
                for j in range(TILES):
                    tile(g, j)
            for g in range(NB - 1, NBT):
                for j in range(TILES):
                    tile(g, j)

        def columns(par, d):
            return s32[par][:, d if par == 0 else d % 4, :]

        def turn_bank(l, m):
            return (psT if m % 4 < 2 else (psB, psA)[l])[:, m % 2, :]

        block = ctx.enter_context(nc.Block())

        @block.sync
        def _(sp):
            def load_idx(g, par):
                if isinstance(g, int):
                    row = x_txt[g:g + 1, 0:CW] if par == 0 else x_txt[g:g + 1, CW - 2:T]
                else:
                    row = x_txt[bass.ds(g, 1), 0:CW] if par == 0 else x_txt[bass.ds(g, 1), CW - 2:T]
                sp.dma_start(idx[par][:, :], row.broadcast_to([P, row.shape[1]])).then_inc(ld_idx[par], 16)

            def turn_h(par, half):
                part = slice(4 * half, 4 * half + 4)
                for rows, cols in zip(h_rows, (s_hi[par], s_lo[par])):
                    sp.dma_start_transpose(out=rows[:, part, :, :].rearrange("p a b c -> p (a b) c"),
                                           in_=cols[:, part, :].rearrange("p a b -> p (a b)"))\
                        .then_inc(h_turned[half], 16)

            def turn_z(i, z_cols):
                sp.wait_ge(zlo_ready, i + 1)
                sp.sem_inc(turn_allowed, 1)
                if z_cols is not z_last:
                    after(sp, l2_done, 2 * i)
                    sp.sem_inc(turn_allowed, 1)
                for cols, rows in zip(z_cols, z_rows):
                    sp.dma_start_transpose(out=cols[:, :, :], in_=rows).then_inc(z_turned, 16)

            for half in range(2):
                sp.dma_start(cb_nat[half * V:(half + 1) * V, :], codebook).then_inc(ld_cb, 16)
            load_idx(0, 0)
            load_idx(0, 1)
            for hh in range(2):
                sp.dma_start(ai_nat[:, hh * N:(hh + 1) * N], inv_A_real[hh * H2:(hh + 1) * H2, :]).then_inc(ld_tok, 16)
                sp.dma_start(ai_nat[:, P + hh * N:P + (hh + 1) * N],
                             A_imag[hh * H2:(hh + 1) * H2, :]).then_inc(ld_tok, 16)
                sp.dma_start(b_nat[:, hh * P:(hh + 1) * P],
                             B[hh * H2:(hh + 1) * H2, :, :].rearrange("h n r -> h (n r)")).then_inc(ld_tok, 16)
                sp.dma_start(ein[hh * N:(hh + 1) * N, 0, :],
                             log_dt[hh * H2:(hh + 1) * H2].rearrange("(a h) -> a h", a=1).broadcast_to([N, H2]))\
                    .then_inc(ld_tok, 16)
                sp.dma_start(x_nat.rearrange("p (c q) -> p c q", c=CH)[:, :, hh * P:(hh + 1) * P],
                             x[:, hh * H2:(hh + 1) * H2, :, :].rearrange("c h n r -> h c (n r)"))\
                    .then_inc(ld_x, 16)
            sp.dma_start(sc[:, :], scales.rearrange("(r p) a -> p (r a)", p=P),
                         allow_slow_non_contiguous=True).then_inc(ld_sc, 16)
            for r in range(KT):
                after(sp, mask_summed, r - MB + 1)
                sp.dma_start(mk[r % MB], mask[r * P:(r + 1) * P, :]).then_inc(ld_mk[r % MB], 16)
                sp.dma_start(w1_nat[:, r, :], weight[r * P:(r + 1) * P, :]).then_inc(ld_w[r], 16)
            sp.dma_start(w2hi_i.rearrange("p (r k) -> p r k", r=KT), packed.rearrange("(r p) k -> p r k", p=P)).then_inc(ld_pk, 16)
            def load_ortho(r):
                sp.dma_start(w2_nat(r), ortho[r * P:(r + 1) * P, :]).then_inc(ld_or[r], 16)

            for r in range(2):
                load_ortho(r)
            for half in range(2):
                sp.wait_ge(lo_ready, 4 * half + 4)
                turn_h(0, half)
            for r in range(2, KT):
                if r in (2, 6):
                    sp.wait_ge(w_turned[0], KT if r == 2 else 2 * KT)
                load_ortho(r)

            def text_out(g, j):
                rows = slice(H + j * P, H + (j + 1) * P)
                return out[g, rows, :] if isinstance(g, int) else \
                    out[bass.ds(g, 1), rows, :].rearrange("a p d -> (a p) d")

            def store(g, j):
                i = TILES * g + j
                sp.wait_ge(out_ready, 2 * i + 2)
                dst = out[TILES * (g - NB) + j, 0:H, :] if isinstance(g, int) and g >= NB else text_out(g, j)
                sp.dma_start(dst, hrow[j][:, :]).then_inc(stored[j], 16)

            def tile(g, j):
                i, q = TILES * g + j, 2 * g + j // 2
                if not (isinstance(g, int) and g == 0 and j == 0):
                    turn_z(i - 1, (z_hi, z_lo))
                if j % 2 == 0 and (not isinstance(g, int) or g < NB - 1):
                    sp.wait_ge(hot_ready, 2 * g + j // 2 + 1)
                    load_idx(g + 1, j // 2)
                if j >= 2:
                    store(g, j - 2)
                elif not isinstance(g, int) or g > 0:
                    store(g - 1, j + 2)
                if j % 2 == 1 and makes(g, j) is not None:
                    sp.wait_ge(hrow_ready, i + 1)
                    for half in range(2):
                        sp.wait_ge(lo_ready, KT * (q + 1) + 4 * half + 4)
                        sp.sem_inc(turn_allowed, 1)
                        turn_h((j // 2 + 1) % 2, half)

            whole(sp, tile)
            turn_z(TILES * NBT - 1, z_last)
            store(NBT - 1, 2)
            store(NBT - 1, 3)
            for j in range(TILES):
                sp.wait_ge(stored[j], 16 * (NBT))

        @block.tensor
        def _(pe):
            def lay_row(n, col, bank):
                pe.wait_ge(col_ready, n)
                pe.matmul(bank[0:1, 0, 0:P], col, ident[:, :], start=True, stop=True).then_inc(row_laid, 1)

            def spread_top(n, bank):
                pe.wait_ge(top_ready, n)
                pe.matmul(bank[:, 1, 0:1], ones[0:1, :], one_max[0:1, 0:1], start=True, stop=True)\
                    .then_inc(top_spread, 1)

            def gather(q, d, par):
                n = KT * q + d
                if d == 0:
                    pe.wait_ge(hot_ready, q + 1)
                after(pe, prod_ready, n)
                pe.matmul(psG[:, 0, 0:CW], cb[:, 1 + d * P:1 + (d + 1) * P], hot[par][:, 1:CW + 1],
                          start=True, stop=True)
                pe.matmul(psG[:, 0, CW:2 * CW], cb[:, d * P:(d + 1) * P], hot[par][:, 0:CW],
                          start=True, stop=True).then_inc(c12_done, 1)
                after(pe, enc_ready, n)
                pe.matmul(psG[:, 1, 0:CW], cb[:, 2 + d * P:2 + (d + 1) * P], hot[par][:, 2:CW + 2],
                          start=True, stop=True).then_inc(c0_done, 1)

            def product1(j, h, k):
                off = (j % 2) * P
                hi, lo = s_hi[j // 2][:, k, off:off + P], s_lo[j // 2][:, k, off:off + P]
                wh, wl = (w[:, k, h * HD:(h + 1) * HD] for w in w1)
                pe.matmul(psA[:, h, :], hi, wh, start=(k == 0), stop=False)
                pe.matmul(psA[:, h, :], hi, wl, start=False, stop=False)
                mm = pe.matmul(psA[:, h, :], lo, wh, start=False, stop=(k == KT - 1))
                if k == KT - 1:
                    mm.then_inc(l1_done, 1)

            def layer1(q, i, j, h):
                after(pe, h1_ready, 2 * (i - 1) + h + 1)
                for k in range(KT):
                    if j % 2 == 0 and h == 0:
                        pe.wait_ge(hi_ready, KT * q + k + 1)
                        pe.wait_ge(lo_ready, KT * q + k + 1)
                    product1(j, h, k)

            def product2(h, k, z_cols):
                wh, wl = (w[:, k, h * HD:(h + 1) * HD] for w in w2)
                pe.matmul(psB[:, h, :], z_cols[0][:, k, :], wh, start=(k == 0), stop=False)
                pe.matmul(psB[:, h, :], z_cols[0][:, k, :], wl, start=False, stop=False)
                mm = pe.matmul(psB[:, h, :], z_cols[1][:, k, :], wh, start=False, stop=(k == KT - 1))
                if k == KT - 1:
                    mm.then_inc(l2_done, 1)

            def layer2(i, h, z_cols):
                after(pe, out_ready, 2 * (i - 1) + h + 1)
                if h == 0:
                    pe.wait_ge(z_turned, 32 * (i + 1))
                for k in range(KT):
                    product2(h, k, z_cols)

            def token_group(g):
                pe.wait_ge(uy_ready, g + 1)
                after(pe, tok_ready, 2 * g)
                for u in range(HG):
                    for ri in range(2):
                        mm = pe.matmul(psT[:, u // 4, (u % 4) * P:(u % 4 + 1) * P], U[:, u, ri, :],
                                       Yb[:, u, ri, :, :].rearrange("p a b -> p (a b)"),
                                       start=(ri == 0), stop=(ri == 1))
                    if u % 4 == 3:
                        mm.then_inc(kmm_done, 1)

            def turn_weights(l, nat, before, product):
                for m in range(2 * KT + 3):
                    if m < 2 * KT:
                        half, k = m // KT, m % KT
                        before(m)
                        after(pe, w_lo[l], m - 3)
                        for u in range(4):
                            mm = pe.transpose(turn_bank(l, m)[:, u * P:(u + 1) * P],
                                              nat(half * 4 + u)[:, k * P:(k + 1) * P], ident[:, :])
                        mm.then_inc(w_turned[l], 1)
                    if m >= 3:
                        pe.wait_ge(w_lo[l], m - 2)
                        product((m - 3) // KT, (m - 3) % KT)

            pe.wait_ge(consts, CONSTS)
            lay_row(1, cs[:, 0:1], psA)
            spread_top(1, psA)
            pe.wait_ge(sig_ready, 1)
            for j in range(TILES):
                mm = pe.transpose(psB[:, 0, j * P:(j + 1) * P], sig[:, HD + j * P:HD + (j + 1) * P],
                                  ident[:, :])
            mm.then_inc(sig_turned, 1)
            pe.wait_ge(ld_tok, 16 * 8)
            pe.wait_ge(ld_x, 32)
            small = ident[0:H2, 0:H2]
            for n in range(2):
                pe.transpose(psT[:, 0, n * H2:(n + 1) * H2], ai_nat[:, n * P:(n + 1) * P], small)
            for n in range(2):
                mm = pe.transpose(psT[:, 0, (2 + n) * H2:(3 + n) * H2],
                                  b_nat[:, 0:2 * P].rearrange("p (m r) -> p m r", r=2)[:, :, n], small)
            mm.then_inc(tok_turned, 1)
            for half in range(2):
                for m in range(CH):
                    c, ri = half * (CH // 2) + m // 2, m % 2
                    src = x_nat.rearrange("p (c m r) -> p c m r", c=CH, r=2)[:, c, :, ri]
                    mm = pe.transpose((psT if half == 0 else psB)[:, 1, m * H2:(m + 1) * H2], src, small)
                mm.then_inc(tok_turned, 1)
            pe.wait_ge(cb_ready, 2)
            gather(0, 0, 0)
            for r in range(KT):
                pe.wait_ge(mask_summed, r + 1)
                if r < 2:
                    pe.wait_ge(tok_taken, 2)
                after(pe, mask_read, r - 1)
                pe.matmul(psT[:, r % 2, 0:32], blocks[:, :], mred[:, r % 2, :], start=True, stop=True)\
                    .then_inc(mask_spread, 1)
                if r < KT - 1:
                    gather(0, r + 1, 0)
            lay_row(2, ws[0][:, 0:1], psA)
            spread_top(2, psA)
            pe.wait_ge(centred, KT)
            pe.wait_ge(mask_read, KT)
            pe.wait_ge(tok_taken, 3)
            pe.wait_ge(sig_read, 1)
            pe.wait_ge(lo_ready, KT)
            turn_weights(0, lambda r: w1_nat[:, r, :], lambda m: None, lambda h, k: product1(0, h, k))

            def before_w2(m):
                if m % KT == 0:
                    pe.wait_ge(w2_built, 4 * (m // KT) + 4)
                if m == 2:
                    pe.wait_ge(h1_ready, 4)

            def tile(g, j):
                i, q, kind = TILES * g + j, 2 * g + j // 2, makes(g, j)

                def slot(s):
                    if kind == "text":
                        gather(q + 1, 4 * (j % 2) + s, (j // 2 + 1) % 2)

                first, w2_turns = (isinstance(g, int) and (g, j) == (0, n) for n in range(2))
                second = not (first or w2_turns)
                slot(0)
                if first:
                    layer1(0, 1, 1, 0)
                elif second:
                    layer1(q, i, j, 0)
                if w2_turns:
                    lay_row(3, ws[1][:, 0:1], psT)
                    spread_top(3, psT)
                slot(1)
                if first:
                    layer1(0, 1, 1, 1)
                elif second:
                    layer1(q, i, j, 1)
                if w2_turns:
                    pe.wait_ge(w_scaled[1], 1)
                    pe.wait_ge(z_turned, 32)
                    turn_weights(1, w2_nat, before_w2, lambda h, k: product2(h, k, (z_hi, z_lo)))
                slot(2)
                if second:
                    layer2(i - 1, 0, (z_hi, z_lo))
                group = group_of(g, j)
                slot(3)
                if second:
                    layer2(i - 1, 1, (z_hi, z_lo))
                if group is not None:
                    token_group(group)
                if isinstance(g, int) and (g, j) == (NB - 1, 1):
                    lay_row(4, ks[:, 0:1], psT)
                    spread_top(4, psT)
                    pe.wait_ge(tok_scaled, 1)

            whole(pe, tile)
            last = TILES * NBT - 1
            layer2(last, 0, z_last)
            layer2(last, 1, z_last)

        @block.scalar
        def _(act):
            def gathered(n):
                act.wait_ge(c12_done, n + 1)
                after(act, prod_ready, n)
                act.activation(c1s[:, :], psG[:, 0, 0:CW], ACT.Identity, scale=cs[:, 8:9]).then_inc(c1_ready, 1)

            def high(n, par, d, made, m):
                act.wait_ge(made, m + 1)
                act.activation(s_hi[par][:, d, :], columns(par, d), ACT.Copy).then_inc(hi_ready, 1)

            def ortho_square(r):
                act.wait_ge(ld_or[r], 16)
                after(act, w2_squared, r)
                act.activation(junk, w2_nat(r), ACT.Square, accum_out=squares[:, 1, r:r + 1])\
                    .then_inc(w2_squared, 1)

            PREPARE = {1: (4, 5), 3: (6, 7)}

            def weights_high_part(l, w, m):
                half, k = m // KT, m % KT
                act.wait_ge(w_turned[l], m + 1)
                if l == 1 and 4 <= k and half == 0:
                    act.wait_ge(w2_built, k + 1)
                act.activation(w[0][:, k, half * HD:(half + 1) * HD], turn_bank(l, m), ACT.Identity,
                               scale=ws[l][:, 1:2]).then_inc(w_hi[l], 1)

            def rows_high(g, q, j, i, col):
                for half in range(2):
                    act.wait_ge(h_turned[half], 32 * (q + 1))
                after(act, stored[j], 16 * g)
                act.activation(hrow[j].rearrange("p (a b) -> p a b", a=KT), h_rows[0][:, :, j % 2, :], ACT.Identity,
                               scale=rowscale[:, col:col + 1]).then_inc(hhi_ready, 1)

            def std(l, i):
                act.wait_ge(ln_step[l], LNS * i + LN_VAR)
                act.activation(ln[l][:, 5:6], mv[l][:, 1:2], ACT.Sqrt, bias=eps[:, :])\
                    .then_inc(std_ready[l], 1)

            act.wait_ge(cb_scaled, 1)
            act.activation(cb[:, 2:D + 2], cb_nat[:, :], ACT.Identity, scale=cs[:, 3:4]).then_inc(cb_hi, 1)
            act.activation(cb[:, 0:2], cb_nat[:, D - 2:D], ACT.Identity, scale=cs[:, 3:4]).then_inc(cb_hi, 1)
            act.wait_ge(tok_turned, 1)
            act.activation(ein[:, 1, :], psT[:, 0, 0:H2], ACT.Copy)
            act.activation(prm[:, :, :].rearrange("p a b -> p (a b)"), psT[:, 0, H2:4 * H2], ACT.Copy)\
                .then_inc(tok_taken, 1)
            for half in range(2):
                act.wait_ge(tok_turned, 2 + half)
                act.activation(C[:, half * 4:(half + 1) * 4, :, :].rearrange("p a b c -> p (a b c)"),
                               (psT if half == 0 else psB)[:, 1, :], ACT.Copy).then_inc(tok_taken, 1)
            gathered(0)
            for r in range(KT):
                high(r, 0, r, scanned, r)
                if r < KT - 1:
                    gathered(r + 1)
                act.wait_ge(masked, r + 1)
                act.activation(junk, w1_nat[:, r, :], ACT.Square, accum_out=squares[:, 0, r:r + 1])\
                    .then_inc(w1_squared, 1)
                act.wait_ge(mean_ready, r + 1)
                act.wait_ge(w1_squared, r + 1)
                act.activation(w1_nat[:, r, :], w1_nat[:, r, :], ACT.Identity, bias=nmean[:, r:r + 1])\
                    .then_inc(centred, 1)
            for r in range(2):
                ortho_square(r)
            act.wait_ge(w_scaled[0], 1)
            for m in range(2 * KT):
                if m == 5:
                    rows_high(0, 0, 0, 0, 0)
                elif m == 11:
                    std(0, 0)
                weights_high_part(0, w1, m)
            for r in range(2, 4):
                ortho_square(r)

            def tile(g, j):
                i, q, kind = TILES * g + j, 2 * g + j // 2, makes(g, j)
                text, par = text_batch(g), (j // 2 + 1) % 2
                col = j if text else TILES

                def slot_in(s):
                    d = 4 * (j % 2) + s
                    if kind == "text":
                        gathered(KT * (q + 1) + d)
                    elif kind == "token":
                        c = 2 * (q + 1 - 2 * NB)
                        act.wait_ge(tok_scaled, 1)
                        act.wait_ge(l1_done, 2 * i)
                        act.wait_ge(lo_ready, KT * (q + 1) + d - 3)
                        act.activation(columns(par, d), tok[:, d, c:c + 2, :].rearrange("p a b -> p (a b)"),
                                       ACT.Identity, scale=ks[:, 1:2]).then_inc(tok_copied, 1)

                def slot_out(s):
                    d = 4 * (j % 2) + s
                    if kind == "text":
                        high(KT * (q + 1) + d, par, d, scanned, KT * (q + 1) + d)
                    elif kind == "token":
                        high(KT * (q + 1) + d, par, d, tok_copied, KT * (q + 1 - 2 * NB) + d)

                def normalised():
                    act.wait_ge(ln_step[1], LNS * i + LN_OUT)
                    after(act, zlo_ready, i)
                    act.activation(z[:, :], hrow[j][:, :], ACT.Identity, bias=ln[1][:, 4:5],
                                   scale=ln[1][:, 3:4]).then_inc(z_ready, 1)
                    after(act, z_turned, 32 * i)
                    act.wait_ge(z_ready, i + 1)
                    act.activation(z_rows[0], z[:, :], ACT.Copy, scale=ZS).then_inc(zhi_ready, 1)

                def prepare(s):
                    if isinstance(g, int) and g == 0 and j == 0:
                        for r in PREPARE.get(s, ()):
                            ortho_square(r)

                slot_in(0)
                tile00 = isinstance(g, int) and (g, j) == (0, 0)
                if not tile00:
                    rows_high(g, q, j, i, col)
                slot_out(0)
                std(1 if tile00 else 0, i)
                slot_in(1)
                slot_out(1)
                prepare(1)
                if isinstance(g, int) and g == 0 and j == 1:
                    act.wait_ge(w_scaled[1], 1)
                    for m in range(2 * KT):
                        weights_high_part(1, w2, m)
                        if m == 12:
                            act.wait_ge(base_ready, 1)
                            act.activation(tmp[3], tmp[0], ACT.Sin)
                            act.activation(tmp[4], tmp[0], ACT.Sin, scale=0.5).then_inc(sines, 1)
                if tile00:
                    normalised()
                slot_in(2)
                if not tile00:
                    std(1, i)
                slot_out(2)
                if not tile00:
                    normalised()
                slot_in(3)
                slot_out(3)
                prepare(3)
                group = group_of(g, j)
                if group is not None:
                    for b in range(2):
                        act.wait_ge(kmm_done, 2 * group + b + 1)
                        first = HG * group + 4 * b
                        act.activation(
                            tok_heads[:, :, :, bass.ds(first, 4)].rearrange("p m a u -> p u a m"),
                            psT[:, b, :].rearrange("p (u a m) -> p u a m", u=4, a=2), ACT.Copy)\
                            .then_inc(tok_ready, 1)

            whole(act, tile)

        @block.vector
        def _(dve):
            steps = [0]

            def link(ins):
                steps[0] += 1
                ins.then_inc(dstep, 1)
                dve.wait_ge(dstep, steps[0])

            def power_of_two(out, in_):
                link(dve.tensor_scalar(out.bitcast(I32), in_.bitcast(I32), EXPONENT, None, ALU.bitwise_and))

            def spread_max(n, bank):
                dve.wait_ge(row_laid, n)
                dve.tensor_reduce(one_max[0:1, 0:1], bank[0:1, 0, 0:P], AX.X, ALU.max).then_inc(top_ready, 1)
                dve.wait_ge(top_spread, n)

            def weight_scale(l):
                w = ws[l]
                spread_max(2 + l, (psA, psT)[l])
                link(dve.tensor_scalar(w[:, 3:4], (psA, psT)[l][:, 1, 0:1], 1e-30, None, ALU.max))
                link(dve.tensor_scalar(w[:, 4:5].bitcast(I32), w[:, 3:4].bitcast(I32), 1, None,
                                       ALU.logical_shift_right))
                link(dve.tensor_scalar(w[:, 5:6].bitcast(I32), w[:, 4:5].bitcast(I32), -1.0, RSQRT,
                                       ALU.mult, ALU.add))
                dve.tensor_scalar(w[:, 1:2].bitcast(I32), w[:, 5:6].bitcast(I32), EXPONENT, None,
                                  ALU.bitwise_and).then_inc(w_scaled[l], 1)
                dve.wait_ge(w_scaled[l], 1)
                link(dve.reciprocal(w[:, 2:3], w[:, 1:2]))
                if l == 1:
                    link(dve.tensor_scalar(w[:, 7:8], w[:, 2:3], 1.0 / ZS, None, ALU.mult))

            def weights_low(l, w, between):
                for m in range(2 * KT):
                    half, k = m // KT, m % KT
                    between(m)
                    dve.wait_ge(w_hi[l], m + 1)
                    part = slice(half * HD, (half + 1) * HD)
                    dve.scalar_tensor_tensor(out=w[1][:, k, part], in0=turn_bank(l, m), scalar=ws[l][:, 1:2],
                                             in1=w[0][:, k, part], op0=ALU.mult, op1=ALU.subtract)\
                        .then_inc(w_lo[l], 1)

            def one_hot(q, par):
                cols = CW if par == 0 else CW + 2
                loaded = 16 * (q // 2 + 1) if isinstance(q, int) else 16 * batch_of[0]
                dve.wait_ge(ld_idx[par], loaded)
                after(dve, c0_done, KT * (q - 1))
                dve.tensor_scalar(hot[par][:, CW + 2 - cols:CW + 2], idx[par][:, :], pidf[:, 0:1], None,
                                  ALU.is_equal).then_inc(hot_ready, 1)

            batch_of = [None]

            def encode(q, d, par, i):
                n = KT * q + d
                dve.wait_ge(c1_ready, n + 1)
                dve.tensor_tensor(prod[:, :], c1s[:, :], psG[:, 0, CW:2 * CW], ALU.mult).then_inc(prod_ready, 1)
                dve.wait_ge(prod_ready, n + 1)
                dve.wait_ge(c0_done, n + 1)
                dve.scalar_tensor_tensor(out=prod[:, :], in0=prod[:, :], scalar=cs[:, 9:10], in1=psG[:, 1, 0:CW],
                                         op0=ALU.add, op1=ALU.mult).then_inc(enc_ready, 1)
                dve.wait_ge(enc_ready, n + 1)
                if i is not None and d % 4 == 0:
                    after(dve, l1_done, 2 * i)
                if par == 1:
                    dve.wait_ge(scanned, n - KT + 1)
                dve.tensor_tensor_scan(columns(par, d), decay[:, :], prod[:, :],
                                       0.0 if par == 0 else s32[0][:, d, CW - 1:CW],
                                       ALU.mult, ALU.add).then_inc(scanned, 1)

            def low(n, par, d):
                dve.wait_ge(hi_ready, n + 1)
                dve.tensor_tensor(s_lo[par][:, d, :], columns(par, d), s_hi[par][:, d, :], ALU.subtract)\
                    .then_inc(lo_ready, 1)

            dve.wait_ge(ld_cb, 32)
            dve.tensor_reduce(cs[:, 0:1], cb_nat[:, :], AX.X, ALU.max, apply_absolute_value=True)\
                .then_inc(col_ready, 1)
            dve.wait_ge(consts, CONSTS)
            link(dve.tensor_tensor_scan(sig[:, HD:HD + CW], decay[:, :], sig[:, 0:CW], 0.0, ALU.mult, ALU.add))
            dve.tensor_tensor_scan(sig[:, HD + CW:D], decay[:, :], sig[:, CW:HD], sig[:, HD + CW - 1:HD + CW],
                                   ALU.mult, ALU.add).then_inc(sig_ready, 1)
            dve.wait_ge(consts, CONSTS)
            for par in range(2):
                link(dve.memset(hot[par][:, 0:2], 0.0))
            one_hot(0, 0)
            spread_max(1, psA)
            link(dve.tensor_scalar(cs[:, 1:2], psA[:, 1, 0:1], 1e-30, None, ALU.max))
            link(dve.reciprocal(cs[:, 2:3], cs[:, 1:2]))
            link(dve.tensor_scalar(cs[:, 4:5], cs[:, 2:3], TOP, None, ALU.mult))
            power_of_two(cs[:, 3:4], cs[:, 4:5])
            link(dve.reciprocal(cs[:, 5:6], cs[:, 3:4]))
            cb_scale_steps = steps[0]
            link(dve.tensor_scalar(cs[:, 6:7], cs[:, 1:2], cs[:, 1:2], 0.7, ALU.mult, ALU.mult))
            link(dve.tensor_scalar(cs[:, 6:7], cs[:, 6:7], 0.3, cs[:, 1:2], ALU.add, ALU.mult))
            link(dve.reciprocal(cs[:, 7:8], cs[:, 6:7]))
            link(dve.tensor_scalar(cs[:, 7:8], cs[:, 7:8], TOP * (1 - DECAY), None, ALU.mult))
            power_of_two(cs[:, 7:8], cs[:, 7:8])
            link(dve.tensor_tensor(cs[:, 10:11], cs[:, 7:8], cs[:, 5:6], ALU.mult))
            link(dve.tensor_scalar(cs[:, 9:10], cs[:, 10:11], 0.3, None, ALU.mult))
            link(dve.tensor_scalar(cs[:, 11:12], cs[:, 10:11], cs[:, 5:6], 0.7, ALU.mult, ALU.mult))
            dve.tensor_tensor(cs[:, 8:9], cs[:, 11:12], cs[:, 5:6], ALU.mult).then_inc(cb_scaled, 1)
            for n, (to, of) in enumerate(((slice(2, D + 2), slice(0, D)), (slice(0, 2), slice(D - 2, D)))):
                dve.wait_ge(cb_hi, n + 1)
                dve.scalar_tensor_tensor(out=cb[V:P, to], in0=cb_nat[V:P, of], scalar=cs[V:P, 3:4],
                                         in1=cb[V:P, to], op0=ALU.mult, op1=ALU.subtract).then_inc(cb_ready, 1)
            dve.wait_ge(sig_turned, 1)
            link(dve.tensor_scalar(rowscale[:, 0:TILES], psB[:, 0, :].rearrange("p (j t) -> p j t", j=TILES)[:, :, 0],
                                   cs[:, 7:8], None, ALU.mult))
            dve.reciprocal(rowscale[:, 0:TILES], rowscale[:, 0:TILES]).then_inc(sig_read, 1)

            for r in range(KT):
                dve.wait_ge(ld_mk[r % MB], 16 * (r // MB + 1))
                after(dve, mask_spread, r - 1)
                dve.tensor_reduce(mred[:, r % 2, :], mk[r % MB].rearrange("p (b w) -> p b w", w=32), AX.X,
                                  ALU.add).then_inc(mask_summed, 1)
                encode(0, r, 0, None)
                dve.wait_ge(mask_spread, r + 1)
                after(dve, masked, r - 1)
                dve.tensor_scalar(bmask[:, r % 2, :], psT[:, r % 2, 0:32], 0.0, None, ALU.is_gt)\
                    .then_inc(mask_read, 1)
                dve.wait_ge(mask_read, r + 1)
                dve.wait_ge(ld_w[r], 16)
                wr = w1_nat[:, r, :].rearrange("p (b w) -> p b w", w=32)
                dve.scalar_tensor_tensor(out=wr, in0=wr, scalar=1.0,
                                         in1=bmask[:, r % 2, :].unsqueeze(2).to_broadcast([P, 32, 32]),
                                         op0=ALU.mult, op1=ALU.mult, accum_out=sums[:, r:r + 1])\
                    .then_inc(masked, 1)
                dve.wait_ge(masked, r + 1)
                dve.tensor_scalar(nmean[:, r:r + 1], sums[:, r:r + 1], -1.0 / D, None, ALU.mult)\
                    .then_inc(mean_ready, 1)
                low(r, 0, r)
            dve.wait_ge(w1_squared, KT)
            dve.tensor_reduce(ws[0][:, 0:1], squares[:, 0, :], AX.X, ALU.max).then_inc(col_ready, 1)
            weight_scale(0)
            dve.wait_ge(sig_read, 1)
            link(dve.tensor_scalar(rowcoef[:, 0:TILES], rowscale[:, 0:TILES], ws[0][:, 2:3], None, ALU.mult))

            def build(r):
                dve.wait_ge(w2_squared, r + 1)
                pair = w2_nat(r).rearrange("p (m b) -> p m b", b=2)
                for b, nib in enumerate((w2lo_i, w2hi_i)):
                    ins = dve.scalar_tensor_tensor(out=pair[:, :, b], in0=nib[:, r * HD:(r + 1) * HD],
                                                   scalar=sc28[:, r:r + 1], in1=pair[:, :, b],
                                                   op0=ALU.mult, op1=ALU.add)
                ins.then_inc(w2_built, 1)

            def normalise(l, i, scale_col):
                w, s, base = ln[l], ln_step[l], LNS * i
                dve.wait_ge(std_ready[l], i + 1)
                if l == 1:
                    after(dve, z_ready, i)
                dve.reciprocal(w[:, 1:2], w[:, 5:6]).then_inc(s, 1)
                dve.wait_ge(s, base + 5)
                dve.scalar_tensor_tensor(out=w[:, 2:3], in0=w[:, 1:2], scalar=w[:, 1:2], in1=w[:, 0:1],
                                         op0=ALU.mult, op1=ALU.mult).then_inc(s, 1)
                dve.wait_ge(s, base + 6)
                dve.scalar_tensor_tensor(out=w[:, 3:4], in0=w[:, 2:3], scalar=1.5, in1=w[:, 1:2],
                                         op0=ALU.add, op1=ALU.mult).then_inc(s, 1)
                dve.wait_ge(s, base + 7)
                if l == 0:
                    dve.tensor_tensor(w[:, 4:5], w[:, 3:4], scale_col, ALU.mult).then_inc(s, 1)
                else:
                    dve.scalar_tensor_tensor(out=w[:, 4:5], in0=w[:, 3:4], scalar=-1.0, in1=mv[1][:, 0:1],
                                             op0=ALU.mult, op1=ALU.mult).then_inc(s, 1)

            def statistics(l, i, j):
                s, base = ln_step[l], LNS * i
                for h in range(2):
                    if l == 0:
                        dve.wait_ge(hrow_ready, i + 1)
                    else:
                        dve.wait_ge(h1_ready, 2 * i + h + 1)
                    dve.bn_stats(bn[l][:, h, :], hrow[j][:, h * HD:(h + 1) * HD]).then_inc(s, 1)
                dve.wait_ge(s, base + 2)
                dve.memset(ln[l][:, 6:7], 0.0)
                dve.bn_aggr(mv[l][:, :], bn[l][:, :, :].rearrange("p a b -> p (a b)")).then_inc(s, 1)
                dve.wait_ge(s, base + 3)
                dve.tensor_scalar(ln[l][:, 0:1], mv[l][:, 1:2], EPS, -0.5, ALU.add, ALU.mult).then_inc(s, 1)

            def finish(i, j, h):
                dve.wait_ge(l2_done, 2 * i + h + 1)
                part = hrow[j][:, h * HD:(h + 1) * HD]
                dve.scalar_tensor_tensor(out=part, in0=psB[:, h, :], scalar=ws[1][:, 7:8], in1=part,
                                         op0=ALU.mult, op1=ALU.add).then_inc(out_ready, 1)

            def z_low(i):
                dve.wait_ge(zhi_ready, i + 1)
                dve.scalar_tensor_tensor(out=z_rows[1], in0=z[:, :], scalar=ZS, in1=z_rows[0],
                                         op0=ALU.mult, op1=ALU.subtract).then_inc(zlo_ready, 1)

            def rows_low(j, i, col):
                dve.wait_ge(hhi_ready, i + 1)
                rows = hrow[j].rearrange("p (a b) -> p a b", a=KT)
                dve.scalar_tensor_tensor(out=rows, in0=h_rows[1][:, :, j % 2, :], scalar=rowscale[:, col:col + 1],
                                         in1=rows, op0=ALU.mult, op1=ALU.add).then_inc(hrow_ready, 1)

            def residual(i, j, h):
                if h == 0:
                    dve.wait_ge(ln_step[0], LNS * i + LN_OUT)
                dve.wait_ge(l1_done, 2 * i + h + 1)
                part = hrow[j][:, h * HD:(h + 1) * HD]
                dve.scalar_tensor_tensor(out=part, in0=psA[:, h, :], scalar=ln[0][:, 4:5], in1=part,
                                         op0=ALU.mult, op1=ALU.add).then_inc(h1_ready, 1)

            def between(m):
                if m == 3:
                    one_hot(1, 1)
                    dve.wait_ge(ld_sc, 16)
                    dve.tensor_scalar(sc28[:, :], sc[:, :], 2.0 ** -28, None, ALU.mult).then_inc(nibbles, 1)
                elif m == 5:
                    dve.wait_ge(ld_pk, 16)
                    dve.tensor_scalar(w2hi_i, w2hi_i, 0x88, None, ALU.bitwise_xor).then_inc(nibbles, 1)
                elif m == 7:
                    rows_low(0, 0, 0)
                elif m == 9:
                    statistics(0, 0, 0)
                elif m == 13:
                    normalise(0, 0, rowcoef[:, 0:1])
                    residual(0, 0, 0)

            def between_w2(m):
                if 1 <= m <= 4:
                    build(3 + m)
                elif m == 12:
                    dve.wait_ge(base_ready, 1)
                    dve.reciprocal(norm[:, :], norm[:, :]).then_inc(norm_ready, 1)

            weights_low(0, w1, between)
            residual(0, 0, 1)
            statistics(1, 0, 0)
            dve.wait_ge(nibbles, 2)
            dve.tensor_scalar(w2lo_i, w2hi_i, 28, None, ALU.logical_shift_left).then_inc(nibbles, 1)
            dve.wait_ge(nibbles, 3)
            dve.tensor_scalar(w2hi_i, w2hi_i, 4, 28, ALU.logical_shift_right, ALU.logical_shift_left)\
                .then_inc(nibbles, 1)
            dve.wait_ge(nibbles, 4)

            def tile(g, j):
                i, q, kind = TILES * g + j, 2 * g + j // 2, makes(g, j)
                text, par = text_batch(g), (j // 2 + 1) % 2
                first = isinstance(g, int) and g == 0
                batch_of[0] = g + 2

                def slot_in(s):
                    if kind == "text":
                        encode(q + 1, 4 * (j % 2) + s, par, i)

                def slot_out(s):
                    if kind is not None:
                        low(KT * (q + 1) + 4 * (j % 2) + s, par, 4 * (j % 2) + s)

                def build_one(r):
                    if isinstance(g, int) and (g, j) == (0, 0):
                        build(r)

                if not first or j >= 2:
                    finish(i - 2, (j + 2) % 4, 1)
                slot_in(0)
                if first and j == 1:
                    weight_scale(1)
                col = j if text else TILES
                if not first or j > 0:
                    rows_low(j, i, col)
                    statistics(0, i, j)
                slot_out(0)
                build_one(0)
                if not first or j > 0:
                    normalise(0, i, rowcoef[:, col:col + 1])
                if not first or j > 0:
                    residual(i, j, 0)
                slot_in(1)
                slot_out(1)
                if not first or j > 0:
                    residual(i, j, 1)
                    statistics(1, i, j)
                else:
                    normalise(1, i, None)
                    build(1)
                if first and j == 1:
                    weights_low(1, w2, between_w2)
                slot_in(2)
                if not first or j > 0:
                    normalise(1, i, None)
                slot_out(2)
                if j % 2 == 1 and (not isinstance(g, int) or q + 2 < 2 * NB):
                    one_hot(q + 2, j // 2)
                if not first or j >= 1:
                    finish(i - 1, (j + 3) % 4, 0)
                z_low(i)
                build_one(2)
                slot_in(3)
                slot_out(3)
                if first and j == 0:
                    build(3)
                    dve.wait_ge(w2_squared, KT)
                    link(dve.tensor_scalar(sq8[:, :], sc[:, :], 8.0, None, ALU.mult))
                    link(dve.tensor_tensor(sq8[:, :], sq8[:, :], sq8[:, :], ALU.mult))
                    link(dve.tensor_tensor(sq8[:, :], sq8[:, :], squares[:, 1, :], ALU.add))
                    dve.tensor_reduce(ws[1][:, 0:1], sq8[:, :], AX.X, ALU.max).then_inc(col_ready, 1)
                group = group_of(g, j)
                if group is not None:
                    dve.wait_ge(tok_ready, 2 * group + 2)
                    dve.tensor_reduce(kmax[:, bass.ds(group, 1)], tok_heads[:, :, :, bass.ds(HG * group, HG)],
                                      AX.XYZ, ALU.max, apply_absolute_value=True).then_inc(kmax_ready, 1)
                if isinstance(g, int) and (g, j) == (NB - 1, 1):
                    dve.wait_ge(kmax_ready, GROUPS)
                    dve.tensor_reduce(ks[:, 0:1], kmax[:, :], AX.X, ALU.max).then_inc(col_ready, 1)
                    spread_max(4, psT)
                    link(dve.tensor_scalar(ks[:, 2:3], psT[:, 1, 0:1], 1e-30, None, ALU.max))
                    link(dve.reciprocal(ks[:, 3:4], ks[:, 2:3]))
                    link(dve.tensor_scalar(ks[:, 3:4], ks[:, 3:4], TOP, None, ALU.mult))
                    power_of_two(ks[:, 1:2], ks[:, 3:4])
                    link(dve.reciprocal(rowscale[:, TILES:TILES + 1], ks[:, 1:2]))
                    dve.tensor_tensor(rowcoef[:, TILES:TILES + 1], rowscale[:, TILES:TILES + 1], ws[0][:, 2:3],
                                      ALU.mult).then_inc(tok_scaled, 1)

            whole(dve, tile)
            last = TILES * NBT - 1
            finish(last - 1, 2, 1)
            finish(last, 3, 0)
            finish(last, 3, 1)

        @block.gpsimd
        def _(pool):
            made = [0]

            def const(ins):
                made[0] += 1
                ins.then_inc(consts, 1)
                pool.wait_ge(consts, made[0])

            const(pool.memset(ident[:, :], 0.0))
            const(pool.affine_select(out=ident[:, :], in_=ident[:, :], compare_op=ALU.not_equal, fill=1.0, base=0,
                                     pattern=[[-1, P]], channel_multiplier=1))
            const(pool.memset(decay[:, :], DECAY))
            const(pool.memset(sig[:, 0:HD], 1.0))
            const(pool.memset(ones[:, :], 1.0))
            const(pool.memset(eps[:, :], EPS))
            for half in range(2):
                const(pool.iota(pid[half * V:(half + 1) * V, :], pattern=[[0, 1]], base=0, channel_multiplier=1))
            const(pool.tensor_copy(pidf[:, :], pid[:, :]))
            const(pool.memset(blocks[:, :], 1.0))
            const(pool.affine_select(out=blocks[:, :].rearrange("p (a b) -> p a b", b=32),
                                     in_=blocks[:, :].rearrange("p (a b) -> p a b", b=32), compare_op=ALU.is_ge,
                                     fill=0.0, base=0, pattern=[[-32, 4], [0, 32]], channel_multiplier=1))
            const(pool.affine_select(out=blocks[:, :].rearrange("p (a b) -> p a b", b=32),
                                     in_=blocks[:, :].rearrange("p (a b) -> p a b", b=32), compare_op=ALU.is_ge,
                                     fill=0.0, base=31, pattern=[[32, 4], [0, 32]], channel_multiplier=-1))
            assert made[0] == CONSTS

            count = [0]

            def link(ins):
                count[0] = count[0] + 1
                ins.then_inc(pool_step, 1)
                pool.wait_ge(pool_step, count[0])

            def ts(out, in_, s1, op0, s2=None, op1=ALU.bypass):
                link(pool.tensor_scalar(out, in_, s1, s2, op0, op1) if s2 is not None
                     else pool.tensor_scalar(out, in_, s1, None, op0))

            def tt(out, a, b, op):
                link(pool.tensor_tensor(out, a, b, op))

            def exp(dst, src, k, r, p):
                ts(src, src, 87.0, ALU.min, -87.0, ALU.max)
                ts(k, src, LOG2E, ALU.mult, MAGIC, ALU.add)
                ts(k, k, -MAGIC, ALU.add)
                ts(r, k, -LN2_HI, ALU.mult)
                tt(r, r, src, ALU.add)
                ts(p, k, -LN2_LO, ALU.mult)
                tt(r, r, p, ALU.add)
                ts(p, r, EXP_POLY[0], ALU.mult, EXP_POLY[1], ALU.add)
                for c in EXP_POLY[2:]:
                    tt(p, p, r, ALU.mult)
                    ts(p, p, c, ALU.add)
                ts(k.bitcast(I32), k, 127.0, ALU.add, float(2 ** 23), ALU.mult)
                tt(dst, p, k, ALU.mult)

            pool.wait_ge(tok_taken, 3)
            flat = ein[:, :, :].rearrange("p a b -> p (a b)")
            exp(flat, flat, tmp[0][:, 0:2 * H2], tmp[1][:, 0:2 * H2], tmp[2][:, 0:2 * H2])
            dt_, ea, ai = ein[:, 0, :], ein[:, 1, :], prm[:, 0, :]
            q3 = tmp[0].rearrange("p (j h) -> p j h", j=LOGS)
            x3 = tmp[3].rearrange("p (j h) -> p j h", j=LOGS)
            tt(q3[:, 0, :], ai, dt_, ALU.mult)
            tt(x3[:, 0, :], ea, dt_, ALU.mult)
            ts(x3[:, 0, :], x3[:, 0, :], -1.0, ALU.mult)
            for l in range(1, LOGS):
                ts(q3[:, l, :], q3[:, l - 1, :], 2.0, ALU.mult)
                ts(x3[:, l, :], x3[:, l - 1, :], 2.0, ALU.mult)
            ts(tmp[1], tmp[0], INV_2PI, ALU.mult, MAGIC, ALU.add)
            ts(tmp[1], tmp[1], -MAGIC, ALU.add)
            for part in (PI2_A, PI2_B, PI2_C):
                ts(tmp[2], tmp[1], -part, ALU.mult)
                tt(tmp[0], tmp[0], tmp[2], ALU.add)
            ts(tmp[0], tmp[0], PI_DOWN, ALU.min, -PI_DOWN, ALU.max)
            exp(tmp[5], tmp[3], tmp[1], tmp[2], tmp[4])
            tt(norm[:, :], ea, ea, ALU.mult)
            tt(tmp[1][:, 0:H2], ai, ai, ALU.mult)
            pool.tensor_tensor(norm[:, :], norm[:, :], tmp[1][:, 0:H2], ALU.add).then_inc(base_ready, 1)

            pool.wait_ge(sines, 1)
            zr, zi = (zp[:, n, :, :].rearrange("p a b -> p (a b)") for n in range(2))
            tt(tmp[4], tmp[4], tmp[4], ALU.mult)
            ts(tmp[4], tmp[4], -2.0, ALU.mult, 1.0, ALU.add)
            tt(zr, tmp[4], tmp[5], ALU.mult)
            tt(zi, tmp[3], tmp[5], ALU.mult)
            br, bi = prm[:, 1, :], prm[:, 2, :]
            er, gr, gi, t0, t1 = (tmp[0][:, n * H2:(n + 1) * H2] for n in range(5))
            fr, fi = (tmp[1][:, n * H2:(n + 1) * H2] for n in range(2))
            ts(er, zp[:, 0, 0, :], -1.0, ALU.add)
            ei = zp[:, 1, 0, :]
            tt(t0, er, ea, ALU.mult)
            tt(t1, ei, ai, ALU.mult)
            tt(fr, t1, t0, ALU.subtract)
            tt(t0, er, ai, ALU.mult)
            tt(t1, ei, ea, ALU.mult)
            tt(fi, t0, t1, ALU.add)
            pool.wait_ge(norm_ready, 1)
            tt(fr, fr, norm[:, :], ALU.mult)
            tt(fi, fi, norm[:, :], ALU.mult)
            ts(fr, fr, 2.0, ALU.mult)
            ts(fi, fi, -2.0, ALU.mult)
            tt(t0, fr, br, ALU.mult)
            tt(t1, fi, bi, ALU.mult)
            tt(gr, t0, t1, ALU.subtract)
            tt(t0, fr, bi, ALU.mult)
            tt(t1, fi, br, ALU.mult)
            tt(gi, t0, t1, ALU.add)
            cr, ci = C[:, :, 0, :], C[:, :, 1, :]
            grb, gib = (v.unsqueeze(1).to_broadcast([P, CH, H2]) for v in (gr, gi))
            a0, a1, a2, a3 = (tmp[n][:, 0:CH * H2].rearrange("p (c h) -> p c h", c=CH) for n in (2, 3, 4, 5))
            tt(a0, cr, grb, ALU.mult)
            tt(a1, ci, gib, ALU.mult)
            tt(a2, cr, gib, ALU.mult)
            tt(a3, ci, grb, ALU.mult)
            tt(cr, a0, a1, ALU.subtract)
            tt(a2, a2, a3, ALU.add)
            ts(ci, a2, -1.0, ALU.mult)
            link(pool.memset(yf, 0.0))
            link(pool.memset(U[:, :, 0, 0:1], 1.0))
            link(pool.memset(U[:, :, 1, 0:1], 0.0))
            pool.wait_ge(w2_squared, KT)

            done = count[0]
            GSTEPS = 4 + 4 * LA + 4 * (LOGS - LA) + 1

            def group(g):
                at = [0]

                def signal(ins):
                    at[0] += 1
                    ins.then_inc(pool_step, 1)

                def step(ins):
                    signal(ins)
                    pool.wait_ge(pool_step, done + GSTEPS * g + at[0])

                after(pool, kmm_done, 2 * g)
                heads = bass.ds(HG * g, HG)
                for ri in range(2):
                    signal(pool.tensor_tensor(zg[:, ri, :, :], zp[:, ri, :, heads],
                                              ones[:, 0:LOGS * HG].rearrange("p (a b) -> p a b", a=LOGS), ALU.mult))
                    signal(pool.tensor_copy(Y[:, :, ri, 0, :].rearrange("p h c -> p c h"), C[:, :, ri, heads]))
                pool.wait_ge(pool_step, done + GSTEPS * g + at[0])

                def double(t, src, dst, scratch, l, w, conj):
                    shape = [P, HG, 2, w]
                    zr_, zi_ = (zg[:, n, l, :].unsqueeze(2).unsqueeze(3).to_broadcast(shape) for n in range(2))
                    step(pool.tensor_tensor(dst, src, zr_, ALU.mult))
                    step(pool.tensor_tensor(scratch, src, zi_, ALU.mult))
                    step(pool.tensor_tensor(dst[:, :, 0, :], dst[:, :, 0, :], scratch[:, :, 1, :],
                                            ALU.add if conj else ALU.subtract))
                    step(pool.tensor_tensor(dst[:, :, 1, :], dst[:, :, 1, :], scratch[:, :, 0, :],
                                            ALU.subtract if conj else ALU.add))

                for l in range(LA):
                    w = 2 ** l
                    double(U, U[:, :, :, 0:w], U[:, :, :, w:2 * w], Ut[:, :, :, 0:w], l, w, False)
                y4 = Y[:, :, :, :, :].rearrange("p h r b c -> p h r (b c)")
                for l in range(LA, LOGS):
                    w = CH * 2 ** (l - LA)
                    double(Y, y4[:, :, :, 0:w], y4[:, :, :, w:2 * w], Ut[:, :, :, 0:w], l, w, True)
                one = ones[0:N, 0:KT * CH].unsqueeze(1).unsqueeze(2).to_broadcast([N, HG, 2, KT * CH])
                signal(pool.tensor_tensor(Yb[0:N, :, :, 0, :], y4[0:N, :, :, :], one, ALU.mult))
                pool.tensor_copy(Yb[N:P, :, :, 1, :], y4[N:P, :, :, :]).then_inc(uy_ready, 1)
                assert at[0] == GSTEPS

            group(0)
            with pool.Fori(1, GROUPS) as g:
                group(g)


_INS = ["x", "x_txt", "L0_tok_log_dt", "L0_tok_B", "L0_tok_inv_A_real", "L0_tok_A_imag", "L0_txt_char_codebook",
        "L0_attn_weight", "L0_attn_mask", "L0_ffn_base_packed", "L0_ffn_scales", "L0_ffn_w_ortho"]


def kernel(**inputs):
    import numpy as _np
    import concourse.bacc as _bacc
    from concourse import mybir as _mybir
    from concourse.bass_utils import run_bass_kernel_spmd as _run

    nc = _bacc.Bacc("TRN2", target_bir_lowering=False, num_devices=1)
    arrays, args = {}, []
    for name in _INS:
        a = _np.ascontiguousarray(inputs[name])
        arrays[f"in_{name}"] = a
        args.append(nc.dram_tensor(f"in_{name}", a.shape, _mybir.dt.from_np(a.dtype), kind="ExternalInput").ap())
    heads, times, features = inputs["x"].shape[1], inputs["x_txt"].shape[1], inputs["L0_attn_weight"].shape[0]
    shape = (inputs["x"].shape[0], heads + times, features)
    args.append(nc.dram_tensor("out", shape, _mybir.dt.float32, kind="ExternalOutput").ap())
    fusion_kernel(nc, *args)
    r = _run(nc, [arrays], core_ids=[0])
    return r.results[0]["out"]
```

```python
from contextlib import ExitStack

import concourse.bass as bass
from concourse import mybir

ALU = mybir.AluOpType
ACT = mybir.ActivationFunctionType
AX = mybir.AxisListType
F32 = mybir.dt.float32
F16 = mybir.dt.float16
I32 = mybir.dt.int32

P = 128
EPS = 1e-5
DECAY = 0.95
TOP = float(2 ** 15)
ZS = 1024.0
EXPONENT = 0x7F800000
MAGIC = 12582912.0
LOG2E = 1.4426950408889634
LN2_HI, LN2_LO = 0.693359375, -2.12194440e-4
INV_2PI = 0.15915494309189535
PI2_A = 6.28125
PI2_B = round((6.283185307179586 - PI2_A) * 2 ** 21) / 2 ** 21
PI2_C = 6.283185307179586 - PI2_A - PI2_B
PI_DOWN = 3.1415925
RSQRT = 1597463007.0 + 14 * 2.0 ** 23
EXP_POLY = [1 / 5040, 1 / 720, 1 / 120, 1 / 24, 1 / 6, 0.5, 1.0, 1.0]


def fusion_kernel(nc, x, x_txt, log_dt, B, inv_A_real, A_imag, codebook, weight, mask,
                  packed, scales, ortho, out):
    CH, H, N, _ = x.shape
    NB, T = x_txt.shape
    V, D = codebook.shape
    KT = D // P
    HD = D // 2
    TILES = T // P
    CW = 2 * P
    H2 = H // 2
    HG = 8
    GROUPS = H2 // HG
    LOGS = 10
    CONSTS = 12
    LA = 7
    assert D == 1024 and V == 64 and 2 * V == P and N == 64 and H == P
    assert TILES == 4 and CH % 4 == 0 and GROUPS == NB == 8

    with ExitStack() as ctx:
        def sb(name, shape, dt):
            return ctx.enter_context(nc.sbuf_tensor(name, shape, dt))

        def ps(name, shape, dt):
            return ctx.enter_context(nc.psum_tensor(name, shape, dt))

        def sem(name):
            return ctx.enter_context(nc.semaphore(name))

        w1 = [sb(f"w1_{n}", [P, KT, D], F16) for n in ("hi", "lo")]
        w2 = [sb(f"w2_{n}", [P, KT, D], F16) for n in ("hi", "lo")]
        s32 = [sb("s32_0", [P, KT, CW], F32), sb("s32_1", [P, 4, CW], F32)]
        s_hi = [sb(f"s_hi{n}", [P, KT, CW], F16) for n in range(2)]
        s_lo = [sb(f"s_lo{n}", [P, KT, CW], F16) for n in range(2)]
        tok = sb("tok", [P, KT, CH, H], F32)
        hrow = [sb(f"hrow{n}", [P, D], F32) for n in range(TILES)]
        h_rows = [sb(f"h_rows_{n}", [P, KT, 2, P], F16) for n in ("hi", "lo")]
        z = sb("z", [P, D], F32)
        z_parts = sb("z_parts", [P, 2, D], F16)
        z_rows = [z_parts[:, n, :] for n in range(2)]
        z_hi = sb("z_hi", [P, KT, P], F16)
        z_lo = sb("z_lo", [P, KT, P], F16)
        ident = sb("ident", [P, P], F32)
        ones = sb("ones", [P, P], F32)
        blocks = sb("blocks", [P, P], F32)
        decay = sb("decay", [P, CW], F32)
        cb = sb("cb", [P, D + 2], F16)
        pid = sb("pid", [P, 1], I32)
        pidf = sb("pidf", [P, 1], F32)
        idx = [sb("idx0", [P, CW], I32), sb("idx1", [P, CW + 2], I32)]
        hot = [sb(f"hot{n}", [P, CW + 2], F16) for n in range(2)]
        c1s = sb("c1s", [P, CW], F32)
        prod = sb("prod", [P, CW], F32)
        cs = sb("cs", [P, 16], F32)
        ws = [sb(f"ws{n}", [P, 8], F32) for n in range(2)]
        one_max = sb("one_max", [1, 4], F32)
        rowscale = sb("rowscale", [P, TILES + 1], F32)
        rowcoef = sb("rowcoef", [P, TILES + 1], F32)
        sums = sb("sums", [P, KT], F32)
        nmean = sb("nmean", [P, KT], F32)
        squares = sb("squares", [P, 2, KT], F32)
        mred = sb("mred", [P, 2, 32], F32)
        bmask = sb("bmask", [P, 2, 32], F32)
        sc = sb("sc", [P, KT], F32)
        sc28 = sb("sc28", [P, KT], F32)
        sq8 = sb("sq8", [P, KT], F32)
        kmax = sb("kmax", [P, GROUPS], F32)
        ks = sb("ks", [P, 4], F32)
        eps = sb("eps", [P, 1], F32)
        norm = sb("norm", [P, H2], F32)
        bn = [sb(f"bn{n}", [P, 2, 6], F32) for n in range(2)]
        mv = [sb(f"mv{n}", [P, 2], F32) for n in range(2)]
        ln = [sb(f"ln{n}", [P, 8], F32) for n in range(2)]
        U = sb("U", [P, HG, 2, P], F32)
        Ut = sb("Ut", [P, HG, 2, P // 2], F32)
        Y = sb("Y", [P, HG, 2, KT, CH], F32)
        Yb = sb("Yb", [P, HG, 2, 2, KT * CH], F32)
        C = sb("C", [P, CH, 2, H2], F32)
        ein = sb("ein", [P, 2, H2], F32)
        prm = sb("prm", [P, 3, H2], F32)
        zg = sb("zg", [P, 2, LOGS, HG], F32)
        zp = sb("zp", [P, 2, LOGS, H2], F32)

        psT = ps("psT", [P, 2, HD], F32)
        psA = ps("psA", [P, 2, HD], F32)
        psB = ps("psB", [P, 2, HD], F32)
        psG = ps("psG", [P, 2, HD], F32)

        w1_nat = tok[:, :, :, :].rearrange("p a b c -> p a (b c)")

        def w2_nat(r):
            return hrow[2 + r][:, :] if r < 2 else w1_nat[:, r - 2, :]

        cb_nat = hrow[0]
        junk = Y[:, :, :, :, :].rearrange("p a b c d -> p (a b c d)")
        sig = z
        w2hi_i = w2[0][:, :, :].rearrange("p a b -> p (a b)").bitcast(I32)
        w2lo_i = w2[1][:, :, :].rearrange("p a b -> p (a b)").bitcast(I32)
        MB = 3
        mk = [s32[1][:, :, :].rearrange("p a b -> p (a b)").bitcast(I32),
              z_parts[:, :, :].rearrange("p a b -> p (a b)").bitcast(I32),
              w2[1][:, 0:2, :].rearrange("p a b -> p (a b)").bitcast(I32)]
        tok_heads = tok[:, :, :, :].rearrange("p b c (a h) -> p (b c) a h", a=2)
        x_nat = U[0:H2, :, :, :].rearrange("p a b c -> p (a b c)")
        ai_nat = Yb[0:H2, 0, :, :, :].rearrange("p a b c -> p (a b c)")
        b_nat = Yb[0:H2, 1, :, :, :].rearrange("p a b c -> p (a b c)")
        z_last = [U[:, 4 * n:4 * n + 4, :, :].rearrange("p a b c -> p (a b c)").bitcast(F16)[:, 0:D]
                  .rearrange("p (a b) -> p a b", a=KT) for n in range(2)]
        NT = LOGS * H2
        uf = U[:, :, :, :].rearrange("p a b c -> p (a b c)")
        yf = Yb[:, :, :, :, :].rearrange("p a b c d -> p (a b c d)")
        tmp = [uf[:, n * NT:(n + 1) * NT] for n in range(3)] + [yf[:, n * NT:(n + 1) * NT] for n in range(3)]

        ld_cb, ld_pk, ld_sc, ld_tok, ld_x = (sem(n) for n in ("ld_cb", "ld_pk", "ld_sc", "ld_tok", "ld_x"))
        ld_w = [sem(f"ld_w{r}") for r in range(KT)]
        ld_mk = [sem(f"ld_mk{n}") for n in range(MB)]
        ld_or = [sem(f"ld_or{r}") for r in range(KT)]
        ld_idx = [sem("ld_idx0"), sem("ld_idx1")]
        stored = [sem(f"stored{n}") for n in range(TILES)]
        consts = sem("consts")
        dstep = sem("dstep")
        col_ready, row_laid, top_ready, top_spread = (
            sem(n) for n in ("col_ready", "row_laid", "top_ready", "top_spread"))
        cols_ready, sum_spread = sem("cols_ready"), sem("sum_spread")
        sig_ready, sig_turned, sig_read = sem("sig_ready"), sem("sig_turned"), sem("sig_read")
        cb_scaled, trigram_scaled, cb_hi, cb_ready, tok_bits = (
            sem(n) for n in ("cb_scaled", "trigram_scaled", "cb_hi", "cb_ready", "tok_bits"))
        tok_turned, tok_taken = sem("tok_turned"), sem("tok_taken")
        mask_summed, mask_spread, mask_read = sem("mask_summed"), sem("mask_spread"), sem("mask_read")
        masked, mean_ready, w1_squared, centred = (
            sem(n) for n in ("masked", "mean_ready", "w1_squared", "centred"))
        nibbles, w2_built, w2_squared = (sem(n) for n in ("nibbles", "w2_built", "w2_squared"))
        w_scaled = [sem("w1_scaled"), sem("w2_scaled")]
        w_turned = [sem("w1_turned"), sem("w2_turned")]
        w_hi = [sem("w1_hi_ready"), sem("w2_hi_ready")]
        w_lo = [sem("w1_lo_ready"), sem("w2_lo_ready")]
        hot_ready, c12_done, c0_done = sem("hot_ready"), sem("c12_done"), sem("c0_done")
        c1_ready, prod_ready, enc_ready, scanned = (
            sem(n) for n in ("c1_ready", "prod_ready", "enc_ready", "scanned"))
        hi_ready, lo_ready, tok_copied = sem("hi_ready"), sem("lo_ready"), sem("tok_copied")
        l1_done, h1_ready, l2_done, out_ready = (
            sem(n) for n in ("l1_done", "h1_ready", "l2_done", "out_ready"))
        hhi_ready, hrow_ready, z_ready, zhi_ready, zlo_ready = (
            sem(n) for n in ("hhi_ready", "hrow_ready", "z_ready", "zhi_ready", "zlo_ready"))
        h_turned, z_turned = [sem("h_turned0"), sem("h_turned1")], sem("z_turned")
        turn_allowed = sem("turn_allowed")
        ln_step = [sem("ln1_step"), sem("ln2_step")]
        std_ready = [sem("std1_ready"), sem("std2_ready")]
        LNS, LN_VAR, LN_OUT = 8, 3, 8
        pool_step = sem("pool_step")
        base_ready, norm_ready, sines = sem("base_ready"), sem("norm_ready"), sem("sines")
        uy_ready, kmm_done, tok_ready, kmax_ready, tok_scaled = (
            sem(n) for n in ("uy_ready", "kmm_done", "tok_ready", "kmax_ready", "tok_scaled"))

        def after(eng, s, count):
            if not isinstance(count, int) or count > 0:
                eng.wait_ge(s, count)

        NBT = NB + CH // TILES

        def text_batch(g):
            return not isinstance(g, int) or g < NB

        def makes(g, j):
            if not isinstance(g, int):
                return "text"
            q = 2 * g + j // 2 + 1
            return "text" if q < 2 * NB else "token" if q < 2 * NBT else None

        def group_of(g, j):
            if isinstance(g, int) and g >= NB - 1:
                return NB - 1 if (g, j) == (NB - 1, 1) else None
            return g if j == 3 else None

        def whole(eng, tile):
            for j in range(TILES):
                tile(0, j)
            with eng.Fori(1, NB - 1) as g:
                for j in range(TILES):
                    tile(g, j)
            for g in range(NB - 1, NBT):
                for j in range(TILES):
                    tile(g, j)

        def columns(par, d):
            return s32[par][:, d if par == 0 else d % 4, :]

        def turn_bank(l, m):
            return (psT if m % 4 < 2 else (psB, psA)[l])[:, m % 2, :]

        block = ctx.enter_context(nc.Block())

        @block.sync
        def _(sp):
            def load_idx(g, par):
                if isinstance(g, int):
                    row = x_txt[g:g + 1, 0:CW] if par == 0 else x_txt[g:g + 1, CW - 2:T]
                else:
                    row = x_txt[bass.ds(g, 1), 0:CW] if par == 0 else x_txt[bass.ds(g, 1), CW - 2:T]
                sp.dma_start(idx[par][:, :], row.broadcast_to([P, row.shape[1]])).then_inc(ld_idx[par], 16)

            def turn_h(par, half):
                part = slice(4 * half, 4 * half + 4)
                for rows, cols in zip(h_rows, (s_hi[par], s_lo[par])):
                    sp.dma_start_transpose(out=rows[:, part, :, :].rearrange("p a b c -> p (a b) c"),
                                           in_=cols[:, part, :].rearrange("p a b -> p (a b)"))\
                        .then_inc(h_turned[half], 16)

            def turn_z(i, z_cols):
                sp.wait_ge(zlo_ready, i + 1)
                sp.sem_inc(turn_allowed, 1)
                if z_cols is not z_last:
                    after(sp, l2_done, 2 * i)
                    sp.sem_inc(turn_allowed, 1)
                for cols, rows in zip(z_cols, z_rows):
                    sp.dma_start_transpose(out=cols[:, :, :], in_=rows).then_inc(z_turned, 16)

            def load_w1(r):
                after(sp, mask_summed, r - MB + 1)
                sp.dma_start(mk[r % MB], mask[r * P:(r + 1) * P, :]).then_inc(ld_mk[r % MB], 16)
                sp.dma_start(w1_nat[:, r, :], weight[r * P:(r + 1) * P, :]).then_inc(ld_w[r], 16)

            for half in range(2):
                sp.dma_start(cb_nat[half * V:(half + 1) * V, :], codebook).then_inc(ld_cb, 16)
            load_idx(0, 0)
            load_idx(0, 1)
            load_w1(0)
            for n, v in enumerate((inv_A_real, A_imag)):
                sp.dma_start(ai_nat[:, n * P:(n + 1) * P].rearrange("h (a n) -> h a n", a=2),
                             v.rearrange("(a h) n -> h a n", a=2)).then_inc(ld_tok, 16)
            sp.dma_start(b_nat[:, 0:2 * P].rearrange("h (a n) -> h a n", a=2),
                         B.rearrange("(a h) n r -> h a (n r)", a=2)).then_inc(ld_tok, 16)
            for hh in range(2):
                sp.dma_start(ein[hh * N:(hh + 1) * N, 0, :],
                             log_dt[hh * H2:(hh + 1) * H2].rearrange("(a h) -> a h", a=1).broadcast_to([N, H2]))\
                    .then_inc(ld_tok, 16)
                sp.dma_start(x_nat.rearrange("p (c q) -> p c q", c=CH)[:, :, hh * P:(hh + 1) * P],
                             x[:, hh * H2:(hh + 1) * H2, :, :].rearrange("c h n r -> h c (n r)"))\
                    .then_inc(ld_x, 16)
            sp.dma_start(sc[:, :], scales.rearrange("(r p) a -> p (r a)", p=P),
                         allow_slow_non_contiguous=True).then_inc(ld_sc, 16)
            for r in range(1, KT):
                load_w1(r)
            sp.dma_start(w2hi_i.rearrange("p (r k) -> p r k", r=KT), packed.rearrange("(r p) k -> p r k", p=P))\
                .then_inc(ld_pk, 16)

            def load_ortho(r):
                sp.dma_start(w2_nat(r), ortho[r * P:(r + 1) * P, :]).then_inc(ld_or[r], 16)

            for r in range(2):
                load_ortho(r)
            for half in range(2):
                sp.wait_ge(lo_ready, 4 * half + 4)
                turn_h(0, half)
            for r in range(2, KT):
                if r in (2, 6):
                    sp.wait_ge(w_turned[0], KT if r == 2 else 2 * KT)
                load_ortho(r)

            def text_out(g, j):
                rows = slice(H + j * P, H + (j + 1) * P)
                return out[g, rows, :] if isinstance(g, int) else \
                    out[bass.ds(g, 1), rows, :].rearrange("a p d -> (a p) d")

            def store(g, j):
                i = TILES * g + j
                sp.wait_ge(out_ready, 2 * i + 2)
                dst = out[TILES * (g - NB) + j, 0:H, :] if isinstance(g, int) and g >= NB else text_out(g, j)
                sp.dma_start(dst, hrow[j][:, :]).then_inc(stored[j], 16)

            def tile(g, j):
                i, q = TILES * g + j, 2 * g + j // 2
                if not (isinstance(g, int) and g == 0 and j == 0):
                    turn_z(i - 1, (z_hi, z_lo))
                if j % 2 == 0 and (not isinstance(g, int) or g < NB - 1):
                    sp.wait_ge(hot_ready, 2 * g + j // 2 + 1)
                    load_idx(g + 1, j // 2)
                if j >= 2:
                    store(g, j - 2)
                elif not isinstance(g, int) or g > 0:
                    store(g - 1, j + 2)
                if j % 2 == 1 and makes(g, j) is not None:
                    sp.wait_ge(hrow_ready, i + 1)
                    for half in range(2):
                        sp.wait_ge(lo_ready, KT * (q + 1) + 4 * half + 4)
                        sp.sem_inc(turn_allowed, 1)
                        turn_h((j // 2 + 1) % 2, half)

            whole(sp, tile)
            turn_z(TILES * NBT - 1, z_last)
            store(NBT - 1, 2)
            for h in range(2):
                half = slice(h * HD, (h + 1) * HD)
                sp.wait_ge(out_ready, 2 * (TILES * NBT - 1) + h + 1)
                sp.dma_start(out[CH - 1, 0:H, half], hrow[3][:, half]).then_inc(stored[3], 16)
            for j in range(TILES):
                sp.wait_ge(stored[j], 16 * (NBT + j // 3))

        @block.tensor
        def _(pe):
            def spread_sum(n, cols, bank):
                pe.wait_ge(cols_ready, n)
                pe.matmul(bank[:, 0, 0:KT], ones[:, :], cols, start=True, stop=True).then_inc(sum_spread, 1)

            def gather(q, d, par):
                n = KT * q + d
                if d == 0:
                    pe.wait_ge(hot_ready, q + 1)
                after(pe, prod_ready, n)
                pe.matmul(psG[:, 0, 0:CW], cb[:, 1 + d * P:1 + (d + 1) * P], hot[par][:, 1:CW + 1],
                          start=True, stop=True)
                pe.matmul(psG[:, 0, CW:2 * CW], cb[:, d * P:(d + 1) * P], hot[par][:, 0:CW],
                          start=True, stop=True).then_inc(c12_done, 1)
                after(pe, enc_ready, n)
                pe.matmul(psG[:, 1, 0:CW], cb[:, 2 + d * P:2 + (d + 1) * P], hot[par][:, 2:CW + 2],
                          start=True, stop=True).then_inc(c0_done, 1)

            def product1(j, h, k):
                off = (j % 2) * P
                hi, lo = s_hi[j // 2][:, k, off:off + P], s_lo[j // 2][:, k, off:off + P]
                wh, wl = (w[:, k, h * HD:(h + 1) * HD] for w in w1)
                pe.matmul(psA[:, h, :], hi, wh, start=(k == 0), stop=False)
                pe.matmul(psA[:, h, :], hi, wl, start=False, stop=False)
                mm = pe.matmul(psA[:, h, :], lo, wh, start=False, stop=(k == KT - 1))
                if k == KT - 1:
                    mm.then_inc(l1_done, 1)

            def layer1(q, i, j, h):
                after(pe, h1_ready, 2 * (i - 1) + h + 1)
                for k in range(KT):
                    if j % 2 == 0 and h == 0:
                        pe.wait_ge(hi_ready, KT * q + k + 1)
                        pe.wait_ge(lo_ready, KT * q + k + 1)
                    product1(j, h, k)

            def product2(h, k, z_cols):
                wh, wl = (w[:, k, h * HD:(h + 1) * HD] for w in w2)
                pe.matmul(psB[:, h, :], z_cols[0][:, k, :], wh, start=(k == 0), stop=False)
                pe.matmul(psB[:, h, :], z_cols[0][:, k, :], wl, start=False, stop=False)
                mm = pe.matmul(psB[:, h, :], z_cols[1][:, k, :], wh, start=False, stop=(k == KT - 1))
                if k == KT - 1:
                    mm.then_inc(l2_done, 1)

            def layer2(i, h, z_cols):
                after(pe, out_ready, 2 * (i - 1) + h + 1)
                if h == 0:
                    pe.wait_ge(z_turned, 32 * (i + 1))
                for k in range(KT):
                    product2(h, k, z_cols)

            def token_group(g):
                pe.wait_ge(uy_ready, g + 1)
                after(pe, tok_ready, 2 * g)
                for u in range(HG):
                    for ri in range(2):
                        mm = pe.matmul(psT[:, u // 4, (u % 4) * P:(u % 4 + 1) * P], U[:, u, ri, :],
                                       Yb[:, u, ri, :, :].rearrange("p a b -> p (a b)"),
                                       start=(ri == 0), stop=(ri == 1))
                    if u % 4 == 3:
                        mm.then_inc(kmm_done, 1)

            def turn_weights(l, nat, before, product):
                for m in range(2 * KT + 3):
                    if m < 2 * KT:
                        half, k = m // KT, m % KT
                        before(m)
                        after(pe, w_lo[l], m - 3)
                        for u in range(4):
                            mm = pe.transpose(turn_bank(l, m)[:, u * P:(u + 1) * P],
                                              nat(half * 4 + u)[:, k * P:(k + 1) * P], ident[:, :])
                        mm.then_inc(w_turned[l], 1)
                    if m >= 3:
                        pe.wait_ge(w_lo[l], m - 2)
                        product((m - 3) // KT, (m - 3) % KT)

            def turn_parameters():
                pe.wait_ge(ld_tok, 16 * 5)
                pe.wait_ge(ld_x, 32)
                small = ident[0:H2, 0:H2]
                for n in range(2):
                    pe.transpose(psT[:, 0, n * H2:(n + 1) * H2], ai_nat[:, n * P:(n + 1) * P], small)
                for n in range(2):
                    mm = pe.transpose(psT[:, 0, (2 + n) * H2:(3 + n) * H2],
                                      b_nat[:, 0:2 * P].rearrange("p (m r) -> p m r", r=2)[:, :, n], small)
                mm.then_inc(tok_turned, 1)
                for half in range(2):
                    for m in range(CH):
                        c, ri = half * (CH // 2) + m // 2, m % 2
                        src = x_nat.rearrange("p (c m r) -> p c m r", c=CH, r=2)[:, c, :, ri]
                        mm = pe.transpose((psT if half == 0 else psB)[:, 1, m * H2:(m + 1) * H2], src, small)
                    mm.then_inc(tok_turned, 1)

            pe.wait_ge(consts, CONSTS)
            pe.wait_ge(col_ready, 1)
            pe.matmul(psA[0:1, 0, 0:P], cs[:, 0:1], ident[:, :], start=True, stop=True).then_inc(row_laid, 1)
            pe.wait_ge(top_ready, 1)
            pe.matmul(psA[:, 1, 0:1], ones[0:1, :], one_max[0:1, 0:1], start=True, stop=True)\
                .then_inc(top_spread, 1)
            pe.wait_ge(sig_ready, 1)
            for j in range(TILES):
                mm = pe.transpose(psB[:, 0, j * P:(j + 1) * P], sig[:, HD + j * P:HD + (j + 1) * P],
                                  ident[:, :])
            mm.then_inc(sig_turned, 1)
            pe.wait_ge(cb_ready, 2)
            gather(0, 0, 0)
            for r in range(KT):
                pe.wait_ge(mask_summed, r + 1)
                if r == 0:
                    pe.wait_ge(cb_scaled, 1)
                after(pe, mask_read, r - 1)
                pe.matmul(psA[:, r % 2, 0:32], blocks[:, :], mred[:, r % 2, :], start=True, stop=True)\
                    .then_inc(mask_spread, 1)
                if r == 0:
                    turn_parameters()
                if r < KT - 1:
                    gather(0, r + 1, 0)
            pe.wait_ge(mask_read, KT)
            pe.wait_ge(w1_squared, KT)
            pe.matmul(psA[:, 0, 0:KT], ones[:, :], squares[:, 0, :], start=True, stop=True).then_inc(sum_spread, 1)
            pe.wait_ge(centred, KT)
            pe.wait_ge(mask_read, KT)
            pe.wait_ge(tok_taken, 3)
            pe.wait_ge(sig_read, 1)
            pe.wait_ge(lo_ready, KT)
            turn_weights(0, lambda r: w1_nat[:, r, :], lambda m: None, lambda h, k: product1(0, h, k))

            def before_w2(slot):
                def step(m):
                    if m % KT == 0:
                        pe.wait_ge(w2_built, 4 * (m // KT) + 4)
                    if m == 2:
                        pe.wait_ge(h1_ready, 4)
                    if m in (7, 11):
                        slot(2 + m // 11)
                return step

            def tile(g, j):
                i, q, kind = TILES * g + j, 2 * g + j // 2, makes(g, j)

                def slot(s):
                    if kind == "text":
                        gather(q + 1, 4 * (j % 2) + s, (j // 2 + 1) % 2)

                first, w2_turns = (isinstance(g, int) and (g, j) == (0, n) for n in range(2))
                second = not (first or w2_turns)
                slot(0)
                if first:
                    layer1(0, 1, 1, 0)
                elif second:
                    layer1(q, i, j, 0)
                if w2_turns:
                    spread_sum(1, sq8[:, :], psT)
                slot(1)
                if first:
                    layer1(0, 1, 1, 1)
                elif second:
                    layer1(q, i, j, 1)
                if isinstance(g, int) and (g, j) == (NB - 1, 2):
                    spread_sum(2, kmax[:, :], psT)
                if w2_turns:
                    pe.wait_ge(w_scaled[1], 1)
                    pe.wait_ge(z_turned, 32)
                    turn_weights(1, w2_nat, before_w2(slot), lambda h, k: product2(h, k, (z_hi, z_lo)))
                else:
                    slot(2)
                if second:
                    layer2(i - 1, 0, (z_hi, z_lo))
                group = group_of(g, j)
                if not w2_turns:
                    slot(3)
                if second:
                    layer2(i - 1, 1, (z_hi, z_lo))
                if group is not None:
                    token_group(group)

            whole(pe, tile)
            last = TILES * NBT - 1
            layer2(last, 0, z_last)
            layer2(last, 1, z_last)

        @block.scalar
        def _(act):
            def gathered(n):
                act.wait_ge(c12_done, n + 1)
                after(act, prod_ready, n)
                act.activation(c1s[:, :], psG[:, 0, 0:CW], ACT.Identity, scale=cs[:, 8:9]).then_inc(c1_ready, 1)

            def high(n, par, d, made, m):
                act.wait_ge(made, m + 1)
                act.activation(s_hi[par][:, d, :], columns(par, d), ACT.Copy).then_inc(hi_ready, 1)

            def ortho_square(r):
                act.wait_ge(ld_or[r], 16)
                after(act, w2_squared, r)
                act.activation(junk, w2_nat(r), ACT.Square, accum_out=squares[:, 1, r:r + 1])\
                    .then_inc(w2_squared, 1)

            def weights_high_part(l, w, m):
                half, k = m // KT, m % KT
                act.wait_ge(w_turned[l], m + 1)
                if l == 1 and 4 <= k and half == 0:
                    act.wait_ge(w2_built, k + 1)
                act.activation(w[0][:, k, half * HD:(half + 1) * HD], turn_bank(l, m), ACT.Identity,
                               scale=ws[l][:, 1:2]).then_inc(w_hi[l], 1)

            def rows_high(g, q, j, i, col):
                for half in range(2):
                    act.wait_ge(h_turned[half], 32 * (q + 1))
                after(act, stored[j], 16 * g)
                act.activation(hrow[j].rearrange("p (a b) -> p a b", a=KT), h_rows[0][:, :, j % 2, :], ACT.Identity,
                               scale=rowscale[:, col:col + 1]).then_inc(hhi_ready, 1)

            def std(l, i):
                act.wait_ge(ln_step[l], LNS * i + LN_VAR)
                act.activation(ln[l][:, 5:6], mv[l][:, 1:2], ACT.Sqrt, bias=eps[:, :])\
                    .then_inc(std_ready[l], 1)

            act.wait_ge(cb_scaled, 1)
            act.activation(cb[:, 2:D + 2], cb_nat[:, :], ACT.Identity, scale=cs[:, 3:4]).then_inc(cb_hi, 1)
            act.activation(cb[:, 0:2], cb_nat[:, D - 2:D], ACT.Identity, scale=cs[:, 3:4]).then_inc(cb_hi, 1)
            act.wait_ge(trigram_scaled, 1)
            gathered(0)
            act.wait_ge(tok_turned, 1)
            act.activation(ein[:, 1, :], psT[:, 0, 0:H2], ACT.Copy)
            act.activation(prm[:, :, :].rearrange("p a b -> p (a b)"), psT[:, 0, H2:4 * H2], ACT.Copy)\
                .then_inc(tok_taken, 1)
            for half in range(2):
                act.wait_ge(tok_turned, 2 + half)
                act.activation(C[:, half * 4:(half + 1) * 4, :, :].rearrange("p a b c -> p (a b c)"),
                               (psT if half == 0 else psB)[:, 1, :], ACT.Copy).then_inc(tok_taken, 1)
            for r in range(KT):
                high(r, 0, r, scanned, r)
                if r < KT - 1:
                    gathered(r + 1)
                act.wait_ge(masked, r + 1)
                act.activation(junk, w1_nat[:, r, :], ACT.Square, accum_out=squares[:, 0, r:r + 1])\
                    .then_inc(w1_squared, 1)
                act.wait_ge(mean_ready, r + 1)
                act.wait_ge(w1_squared, r + 1)
                act.activation(w1_nat[:, r, :], w1_nat[:, r, :], ACT.Identity, bias=nmean[:, r:r + 1])\
                    .then_inc(centred, 1)
            act.wait_ge(w_scaled[0], 1)
            for m in range(2 * KT):
                if m == 5:
                    rows_high(0, 0, 0, 0, 0)
                elif m == 8:
                    ortho_square(0)
                elif m == 11:
                    std(0, 0)
                elif m == 13:
                    ortho_square(1)
                weights_high_part(0, w1, m)
            for r in range(2, 6):
                ortho_square(r)

            def tile(g, j):
                i, q, kind = TILES * g + j, 2 * g + j // 2, makes(g, j)
                text, par = text_batch(g), (j // 2 + 1) % 2
                col = j if text else TILES

                def slot_in(s):
                    d = 4 * (j % 2) + s
                    if kind == "text":
                        gathered(KT * (q + 1) + d)
                    elif kind == "token":
                        c = 2 * (q + 1 - 2 * NB)
                        act.wait_ge(tok_scaled, 1)
                        act.wait_ge(l1_done, 2 * i)
                        act.wait_ge(lo_ready, KT * (q + 1) + d - 3)
                        act.activation(columns(par, d), tok[:, d, c:c + 2, :].rearrange("p a b -> p (a b)"),
                                       ACT.Identity, scale=ks[:, 1:2]).then_inc(tok_copied, 1)

                def slot_out(s):
                    d = 4 * (j % 2) + s
                    if kind == "text":
                        high(KT * (q + 1) + d, par, d, scanned, KT * (q + 1) + d)
                    elif kind == "token":
                        high(KT * (q + 1) + d, par, d, tok_copied, KT * (q + 1 - 2 * NB) + d)

                def normalised():
                    act.wait_ge(ln_step[1], LNS * i + LN_OUT)
                    after(act, zlo_ready, i)
                    act.activation(z[:, :], hrow[j][:, :], ACT.Identity, bias=ln[1][:, 4:5],
                                   scale=ln[1][:, 3:4]).then_inc(z_ready, 1)
                    after(act, z_turned, 32 * i)
                    act.wait_ge(z_ready, i + 1)
                    act.activation(z_rows[0], z[:, :], ACT.Copy, scale=ZS).then_inc(zhi_ready, 1)

                if kind != "token":
                    slot_in(0)
                tile00, tile01 = (isinstance(g, int) and (g, j) == (0, n) for n in range(2))
                if not tile00:
                    rows_high(g, q, j, i, col)
                if kind != "token":
                    slot_out(0)
                std(1 if tile00 else 0, i)
                if tile00:
                    for r in range(6, KT):
                        ortho_square(r)
                if tile01:
                    act.wait_ge(base_ready, 1)
                    act.activation(tmp[3], tmp[0], ACT.Sin)
                    act.activation(tmp[4], tmp[0], ACT.Sin, scale=0.5).then_inc(sines, 1)
                if kind == "token":
                    slot_in(0)
                    slot_out(0)
                slot_in(1)
                if not tile01:
                    slot_out(1)
                if tile01:
                    act.wait_ge(w_scaled[1], 1)
                    for m in range(2 * KT):
                        weights_high_part(1, w2, m)
                        if m == 4:
                            slot_out(1)
                        elif m in (7, 11):
                            slot_in(2 + m // 11)
                        elif m in (8, 12):
                            slot_out(2 + m // 12)
                if tile00:
                    normalised()
                if not tile01:
                    slot_in(2)
                if not tile00:
                    std(1, i)
                if not tile01:
                    slot_out(2)
                if not tile00:
                    normalised()
                if not tile01:
                    slot_in(3)
                    slot_out(3)
                group = group_of(g, j)
                if group is not None:
                    for b in range(2):
                        act.wait_ge(kmm_done, 2 * group + b + 1)
                        first = HG * group + 4 * b
                        act.activation(
                            tok_heads[:, :, :, bass.ds(first, 4)].rearrange("p m a u -> p u a m"),
                            psT[:, b, :].rearrange("p (u a m) -> p u a m", u=4, a=2), ACT.Copy)\
                            .then_inc(tok_ready, 1)

            whole(act, tile)

        @block.vector
        def _(dve):
            steps = [0]

            def link(ins):
                steps[0] += 1
                ins.then_inc(dstep, 1)
                dve.wait_ge(dstep, steps[0])

            def power_of_two(out, in_, ready):
                dve.tensor_scalar(out.bitcast(I32), in_.bitcast(I32), EXPONENT, None, ALU.bitwise_and)\
                    .then_inc(ready, 1)

            def weight_scale(l):
                w = ws[l]
                dve.wait_ge(sum_spread, l + 1)
                link(dve.tensor_reduce(w[:, 0:1], (psA, psT)[l][:, 0, 0:KT], AX.X, ALU.add))
                link(dve.tensor_scalar(w[:, 3:4], w[:, 0:1], 1e-30, None, ALU.max))
                link(dve.tensor_scalar(w[:, 4:5].bitcast(I32), w[:, 3:4].bitcast(I32), 1, None,
                                       ALU.logical_shift_right))
                link(dve.tensor_scalar(w[:, 5:6].bitcast(I32), w[:, 4:5].bitcast(I32), -1.0, RSQRT,
                                       ALU.mult, ALU.add))
                power_of_two(w[:, 1:2], w[:, 5:6], w_scaled[l])
                dve.wait_ge(w_scaled[l], 1)
                link(dve.reciprocal(w[:, 2:3], w[:, 1:2]))
                if l == 1:
                    link(dve.tensor_scalar(w[:, 7:8], w[:, 2:3], 1.0 / ZS, None, ALU.mult))

            def weights_low(l, w, between):
                for m in range(2 * KT):
                    half, k = m // KT, m % KT
                    between(m)
                    dve.wait_ge(w_hi[l], m + 1)
                    part = slice(half * HD, (half + 1) * HD)
                    dve.scalar_tensor_tensor(out=w[1][:, k, part], in0=turn_bank(l, m), scalar=ws[l][:, 1:2],
                                             in1=w[0][:, k, part], op0=ALU.mult, op1=ALU.subtract)\
                        .then_inc(w_lo[l], 1)

            def one_hot(q, par):
                cols = CW if par == 0 else CW + 2
                loaded = 16 * (q // 2 + 1) if isinstance(q, int) else 16 * batch_of[0]
                dve.wait_ge(ld_idx[par], loaded)
                after(dve, c0_done, KT * (q - 1))
                dve.tensor_scalar(hot[par][:, CW + 2 - cols:CW + 2], idx[par][:, :], pidf[:, 0:1], None,
                                  ALU.is_equal).then_inc(hot_ready, 1)

            batch_of = [None]

            def encode(q, d, par, i, between=lambda s: None):
                n = KT * q + d
                dve.wait_ge(c1_ready, n + 1)
                dve.tensor_tensor(prod[:, :], c1s[:, :], psG[:, 0, CW:2 * CW], ALU.mult).then_inc(prod_ready, 1)
                between(0)
                dve.wait_ge(prod_ready, n + 1)
                dve.wait_ge(c0_done, n + 1)
                dve.scalar_tensor_tensor(out=prod[:, :], in0=prod[:, :], scalar=cs[:, 9:10], in1=psG[:, 1, 0:CW],
                                         op0=ALU.add, op1=ALU.mult).then_inc(enc_ready, 1)
                between(1)
                dve.wait_ge(enc_ready, n + 1)
                if i is not None and d % 4 == 0:
                    after(dve, l1_done, 2 * i)
                if par == 1:
                    dve.wait_ge(scanned, n - KT + 1)
                dve.tensor_tensor_scan(columns(par, d), decay[:, :], prod[:, :],
                                       0.0 if par == 0 else s32[0][:, d, CW - 1:CW],
                                       ALU.mult, ALU.add).then_inc(scanned, 1)

            def low(n, par, d):
                dve.wait_ge(hi_ready, n + 1)
                dve.tensor_tensor(s_lo[par][:, d, :], columns(par, d), s_hi[par][:, d, :], ALU.subtract)\
                    .then_inc(lo_ready, 1)

            def mask_sum(r):
                dve.wait_ge(ld_mk[r % MB], 16 * (r // MB + 1))
                after(dve, mask_spread, r - 1)
                dve.tensor_reduce(mred[:, r % 2, :], mk[r % MB].rearrange("p (b w) -> p b w", w=32), AX.X,
                                  ALU.add).then_inc(mask_summed, 1)

            dve.wait_ge(ld_cb, 32)
            dve.tensor_reduce(cs[:, 0:1], cb_nat[:, :], AX.X, ALU.max, apply_absolute_value=True)\
                .then_inc(col_ready, 1)
            dve.wait_ge(consts, CONSTS)
            link(dve.tensor_tensor_scan(sig[:, HD:HD + CW], decay[:, :], sig[:, 0:CW], 0.0, ALU.mult, ALU.add))
            dve.tensor_tensor_scan(sig[:, HD + CW:D], decay[:, :], sig[:, CW:HD], sig[:, HD + CW - 1:HD + CW],
                                   ALU.mult, ALU.add).then_inc(sig_ready, 1)
            dve.wait_ge(consts, CONSTS)
            for par in range(2):
                link(dve.memset(hot[par][:, 0:2], 0.0))
            one_hot(0, 0)
            dve.wait_ge(row_laid, 1)
            dve.tensor_reduce(one_max[0:1, 0:1], psA[0:1, 0, 0:P], AX.X, ALU.max).then_inc(top_ready, 1)
            dve.wait_ge(top_spread, 1)
            link(dve.tensor_scalar(cs[:, 1:2], psA[:, 1, 0:1], 1e-30, None, ALU.max))
            link(dve.reciprocal(cs[:, 2:3], cs[:, 1:2]))
            link(dve.tensor_scalar(cs[:, 4:5], cs[:, 2:3], TOP, None, ALU.mult))
            power_of_two(cs[:, 3:4], cs[:, 4:5], cb_scaled)
            dve.wait_ge(cb_scaled, 1)
            link(dve.reciprocal(cs[:, 5:6], cs[:, 3:4]))
            link(dve.tensor_scalar(cs[:, 6:7], cs[:, 1:2], cs[:, 1:2], 0.7, ALU.mult, ALU.mult))
            link(dve.tensor_scalar(cs[:, 6:7], cs[:, 6:7], 0.3, cs[:, 1:2], ALU.add, ALU.mult))
            link(dve.reciprocal(cs[:, 7:8], cs[:, 6:7]))
            link(dve.tensor_scalar(cs[:, 7:8], cs[:, 7:8], TOP * (1 - DECAY), None, ALU.mult))
            power_of_two(cs[:, 7:8], cs[:, 7:8], cb_scaled)
            dve.wait_ge(cb_scaled, 2)
            link(dve.tensor_tensor(cs[:, 10:11], cs[:, 7:8], cs[:, 5:6], ALU.mult))
            link(dve.tensor_scalar(cs[:, 9:10], cs[:, 10:11], 0.3, None, ALU.mult))
            link(dve.tensor_scalar(cs[:, 11:12], cs[:, 10:11], cs[:, 5:6], 0.7, ALU.mult, ALU.mult))
            dve.tensor_tensor(cs[:, 8:9], cs[:, 11:12], cs[:, 5:6], ALU.mult).then_inc(trigram_scaled, 1)
            for n, (to, of) in enumerate(((slice(2, D + 2), slice(0, D)), (slice(0, 2), slice(D - 2, D)))):
                dve.wait_ge(cb_hi, n + 1)
                dve.scalar_tensor_tensor(out=cb[V:P, to], in0=cb_nat[V:P, of], scalar=cs[V:P, 3:4],
                                         in1=cb[V:P, to], op0=ALU.mult, op1=ALU.subtract).then_inc(cb_ready, 1)
            mask_sum(0)
            dve.wait_ge(sig_turned, 1)
            link(dve.tensor_scalar(rowscale[:, 0:TILES], psB[:, 0, :].rearrange("p (j t) -> p j t", j=TILES)[:, :, 0],
                                   cs[:, 7:8], None, ALU.mult))
            dve.reciprocal(rowscale[:, 0:TILES], rowscale[:, 0:TILES]).then_inc(sig_read, 1)

            def between_encoding(r):
                def step(s):
                    if s == 0:
                        dve.wait_ge(mask_spread, r + 1)
                        after(dve, masked, r - 1)
                        dve.tensor_scalar(bmask[:, r % 2, :], psA[:, r % 2, 0:32], 0.0, None, ALU.is_gt)\
                            .then_inc(mask_read, 1)
                    elif r < KT - 1:
                        mask_sum(r + 1)
                return step

            for r in range(KT):
                encode(0, r, 0, None, between_encoding(r))
                dve.wait_ge(mask_read, r + 1)
                dve.wait_ge(ld_w[r], 16)
                wr = w1_nat[:, r, :].rearrange("p (b w) -> p b w", w=32)
                dve.scalar_tensor_tensor(out=wr, in0=wr, scalar=1.0,
                                         in1=bmask[:, r % 2, :].unsqueeze(2).to_broadcast([P, 32, 32]),
                                         op0=ALU.mult, op1=ALU.mult, accum_out=sums[:, r:r + 1])\
                    .then_inc(masked, 1)
                low(r, 0, r)
                dve.wait_ge(masked, r + 1)
                dve.tensor_scalar(nmean[:, r:r + 1], sums[:, r:r + 1], -1.0 / D, None, ALU.mult)\
                    .then_inc(mean_ready, 1)
            weight_scale(0)
            dve.wait_ge(sig_read, 1)
            link(dve.tensor_scalar(rowcoef[:, 0:TILES], rowscale[:, 0:TILES], ws[0][:, 2:3], None, ALU.mult))

            def build(r):
                dve.wait_ge(w2_squared, r + 1)
                pair = w2_nat(r).rearrange("p (m b) -> p m b", b=2)
                for b, nib in enumerate((w2lo_i, w2hi_i)):
                    ins = dve.scalar_tensor_tensor(out=pair[:, :, b], in0=nib[:, r * HD:(r + 1) * HD],
                                                   scalar=sc28[:, r:r + 1], in1=pair[:, :, b],
                                                   op0=ALU.mult, op1=ALU.add)
                ins.then_inc(w2_built, 1)

            def normalise(l, i, scale_col):
                w, s, base = ln[l], ln_step[l], LNS * i
                dve.wait_ge(std_ready[l], i + 1)
                if l == 1:
                    after(dve, z_ready, i)
                dve.reciprocal(w[:, 1:2], w[:, 5:6]).then_inc(s, 1)
                dve.wait_ge(s, base + 5)
                dve.scalar_tensor_tensor(out=w[:, 2:3], in0=w[:, 1:2], scalar=w[:, 1:2], in1=w[:, 0:1],
                                         op0=ALU.mult, op1=ALU.mult).then_inc(s, 1)
                dve.wait_ge(s, base + 6)
                dve.scalar_tensor_tensor(out=w[:, 3:4], in0=w[:, 2:3], scalar=1.5, in1=w[:, 1:2],
                                         op0=ALU.add, op1=ALU.mult).then_inc(s, 1)
                dve.wait_ge(s, base + 7)
                if l == 0:
                    dve.tensor_tensor(w[:, 4:5], w[:, 3:4], scale_col, ALU.mult).then_inc(s, 1)
                else:
                    dve.scalar_tensor_tensor(out=w[:, 4:5], in0=w[:, 3:4], scalar=-1.0, in1=mv[1][:, 0:1],
                                             op0=ALU.mult, op1=ALU.mult).then_inc(s, 1)

            def statistics(l, i, j):
                s, base = ln_step[l], LNS * i
                for h in range(2):
                    if l == 0:
                        dve.wait_ge(hrow_ready, i + 1)
                    else:
                        dve.wait_ge(h1_ready, 2 * i + h + 1)
                    dve.bn_stats(bn[l][:, h, :], hrow[j][:, h * HD:(h + 1) * HD]).then_inc(s, 1)
                dve.wait_ge(s, base + 2)
                dve.memset(ln[l][:, 6:7], 0.0)
                dve.bn_aggr(mv[l][:, :], bn[l][:, :, :].rearrange("p a b -> p (a b)")).then_inc(s, 1)
                dve.wait_ge(s, base + 3)
                dve.tensor_scalar(ln[l][:, 0:1], mv[l][:, 1:2], EPS, -0.5, ALU.add, ALU.mult).then_inc(s, 1)

            def finish(i, j, h):
                dve.wait_ge(l2_done, 2 * i + h + 1)
                part = hrow[j][:, h * HD:(h + 1) * HD]
                dve.scalar_tensor_tensor(out=part, in0=psB[:, h, :], scalar=ws[1][:, 7:8], in1=part,
                                         op0=ALU.mult, op1=ALU.add).then_inc(out_ready, 1)

            def z_low(i):
                dve.wait_ge(zhi_ready, i + 1)
                dve.scalar_tensor_tensor(out=z_rows[1], in0=z[:, :], scalar=ZS, in1=z_rows[0],
                                         op0=ALU.mult, op1=ALU.subtract).then_inc(zlo_ready, 1)

            def rows_low(j, i, col):
                dve.wait_ge(hhi_ready, i + 1)
                rows = hrow[j].rearrange("p (a b) -> p a b", a=KT)
                dve.scalar_tensor_tensor(out=rows, in0=h_rows[1][:, :, j % 2, :], scalar=rowscale[:, col:col + 1],
                                         in1=rows, op0=ALU.mult, op1=ALU.add).then_inc(hrow_ready, 1)

            def residual(i, j, h):
                if h == 0:
                    dve.wait_ge(ln_step[0], LNS * i + LN_OUT)
                dve.wait_ge(l1_done, 2 * i + h + 1)
                part = hrow[j][:, h * HD:(h + 1) * HD]
                dve.scalar_tensor_tensor(out=part, in0=psA[:, h, :], scalar=ln[0][:, 4:5], in1=part,
                                         op0=ALU.mult, op1=ALU.add).then_inc(h1_ready, 1)

            def between(m):
                if m == 3:
                    one_hot(1, 1)
                    dve.wait_ge(ld_sc, 16)
                    dve.tensor_scalar(sc28[:, :], sc[:, :], 2.0 ** -28, None, ALU.mult).then_inc(nibbles, 1)
                elif m == 5:
                    dve.wait_ge(ld_pk, 16)
                    dve.tensor_scalar(w2hi_i, w2hi_i, 0x88, None, ALU.bitwise_xor).then_inc(nibbles, 1)
                elif m == 7:
                    rows_low(0, 0, 0)
                elif m == 9:
                    statistics(0, 0, 0)
                elif m == 13:
                    normalise(0, 0, rowcoef[:, 0:1])
                    residual(0, 0, 0)

            def between_w2(slot_in, slot_out):
                def step(m):
                    if m == 0:
                        slot_in(1)
                    elif 1 <= m <= 4:
                        build(3 + m)
                    elif m == 5:
                        slot_out(1)
                    elif m in (8, 12):
                        slot_in(2 + m // 12)
                    elif m in (9, 13):
                        slot_out(2 + m // 13)
                    elif m == 15:
                        statistics(1, 1, 1)
                return step

            weights_low(0, w1, between)
            residual(0, 0, 1)
            statistics(1, 0, 0)

            def low_nibbles():
                dve.wait_ge(nibbles, 2)
                dve.tensor_scalar(w2lo_i, w2hi_i, 28, None, ALU.logical_shift_left).then_inc(nibbles, 1)

            def high_nibbles():
                dve.wait_ge(nibbles, 3)
                dve.tensor_scalar(w2hi_i, w2hi_i, 4, 28, ALU.logical_shift_right, ALU.logical_shift_left)\
                    .then_inc(nibbles, 1)
                dve.wait_ge(nibbles, 4)

            def tile(g, j):
                i, q, kind = TILES * g + j, 2 * g + j // 2, makes(g, j)
                text, par = text_batch(g), (j // 2 + 1) % 2
                first = isinstance(g, int) and g == 0
                batch_of[0] = g + 2

                def slot_in(s):
                    if kind == "text":
                        encode(q + 1, 4 * (j % 2) + s, par, i)

                def slot_out(s):
                    if kind is not None:
                        low(KT * (q + 1) + 4 * (j % 2) + s, par, 4 * (j % 2) + s)

                if not first or j >= 2:
                    finish(i - 2, (j + 2) % 4, 1)
                slot_in(0)
                if first and j == 1:
                    weight_scale(1)
                col = j if text else TILES
                if not first or j > 0:
                    rows_low(j, i, col)
                    statistics(0, i, j)
                if first and j == 0:
                    low_nibbles()
                if kind != "token":
                    slot_out(0)
                if first and j == 0:
                    high_nibbles()
                    build(0)
                if not first or j > 0:
                    normalise(0, i, rowcoef[:, col:col + 1])
                    residual(i, j, 0)
                if first and j == 1:
                    residual(i, j, 1)
                    dve.wait_ge(base_ready, 1)
                    dve.reciprocal(norm[:, :], norm[:, :]).then_inc(norm_ready, 1)
                if isinstance(g, int) and (g, j) == (NB - 1, 2):
                    dve.wait_ge(sum_spread, 3)
                    link(dve.tensor_reduce(ks[:, 0:1], psT[:, 0, 0:GROUPS], AX.X, ALU.add))
                    link(dve.tensor_scalar(ks[:, 2:3], ks[:, 0:1], 1e-30, None, ALU.max))
                    link(dve.reciprocal(ks[:, 3:4], ks[:, 2:3]))
                    link(dve.tensor_scalar(ks[:, 3:4], ks[:, 3:4], TOP, None, ALU.mult))
                    power_of_two(ks[:, 1:2], ks[:, 3:4], tok_bits)
                    dve.wait_ge(tok_bits, 1)
                    link(dve.reciprocal(rowscale[:, TILES:TILES + 1], ks[:, 1:2]))
                    dve.tensor_tensor(rowcoef[:, TILES:TILES + 1], rowscale[:, TILES:TILES + 1], ws[0][:, 2:3],
                                      ALU.mult).then_inc(tok_scaled, 1)
                if kind == "token":
                    slot_out(0)
                tile01 = first and j == 1
                if not tile01:
                    slot_in(1)
                    slot_out(1)
                if not first or j > 1:
                    residual(i, j, 1)
                    statistics(1, i, j)
                elif j == 0:
                    normalise(1, i, None)
                    build(1)
                    build(2)
                if tile01:
                    weights_low(1, w2, between_w2(slot_in, slot_out))
                else:
                    slot_in(2)
                if not first or j > 0:
                    normalise(1, i, None)
                if not tile01:
                    slot_out(2)
                if j % 2 == 1 and (not isinstance(g, int) or q + 2 < 2 * NB):
                    one_hot(q + 2, j // 2)
                if not first or j >= 1:
                    finish(i - 1, (j + 3) % 4, 0)
                z_low(i)
                if not tile01:
                    slot_in(3)
                    if first and j == 0:
                        build(3)
                    slot_out(3)
                if first and j == 0:
                    dve.wait_ge(w2_squared, KT)
                    link(dve.tensor_scalar(sq8[:, :], sc[:, :], 8.0, None, ALU.mult))
                    link(dve.tensor_tensor(sq8[:, :], sq8[:, :], sq8[:, :], ALU.mult))
                    dve.tensor_tensor(sq8[:, :], sq8[:, :], squares[:, 1, :], ALU.add).then_inc(cols_ready, 1)
                group = group_of(g, j)
                if group is not None:
                    dve.wait_ge(tok_ready, 2 * group + 2)
                    dve.tensor_reduce(kmax[:, bass.ds(group, 1)], tok_heads[:, :, :, bass.ds(HG * group, HG)],
                                      AX.XYZ, ALU.max, apply_absolute_value=True).then_inc(kmax_ready, 1)
                if isinstance(g, int) and (g, j) == (NB - 1, 1):
                    dve.wait_ge(kmax_ready, GROUPS)
                    dve.sem_inc(cols_ready, 1)

            whole(dve, tile)
            last = TILES * NBT - 1
            finish(last - 1, 2, 1)
            finish(last, 3, 0)
            finish(last, 3, 1)

        @block.gpsimd
        def _(pool):
            made = [0]

            def const(ins):
                made[0] += 1
                ins.then_inc(consts, 1)
                pool.wait_ge(consts, made[0])

            const(pool.memset(ident[:, :], 0.0))
            const(pool.affine_select(out=ident[:, :], in_=ident[:, :], compare_op=ALU.not_equal, fill=1.0, base=0,
                                     pattern=[[-1, P]], channel_multiplier=1))
            const(pool.memset(decay[:, :], DECAY))
            const(pool.memset(sig[:, 0:HD], 1.0))
            const(pool.memset(ones[:, :], 1.0))
            const(pool.memset(eps[:, :], EPS))
            for half in range(2):
                const(pool.iota(pid[half * V:(half + 1) * V, :], pattern=[[0, 1]], base=0, channel_multiplier=1))
            const(pool.tensor_copy(pidf[:, :], pid[:, :]))
            const(pool.memset(blocks[:, :], 1.0))
            const(pool.affine_select(out=blocks[:, :].rearrange("p (a b) -> p a b", b=32),
                                     in_=blocks[:, :].rearrange("p (a b) -> p a b", b=32), compare_op=ALU.is_ge,
                                     fill=0.0, base=0, pattern=[[-32, 4], [0, 32]], channel_multiplier=1))
            const(pool.affine_select(out=blocks[:, :].rearrange("p (a b) -> p a b", b=32),
                                     in_=blocks[:, :].rearrange("p (a b) -> p a b", b=32), compare_op=ALU.is_ge,
                                     fill=0.0, base=31, pattern=[[32, 4], [0, 32]], channel_multiplier=-1))
            assert made[0] == CONSTS

            count = [0]

            def link(ins):
                count[0] = count[0] + 1
                ins.then_inc(pool_step, 1)
                pool.wait_ge(pool_step, count[0])

            def ts(out, in_, s1, op0, s2=None, op1=ALU.bypass):
                link(pool.tensor_scalar(out, in_, s1, s2, op0, op1) if s2 is not None
                     else pool.tensor_scalar(out, in_, s1, None, op0))

            def tt(out, a, b, op):
                link(pool.tensor_tensor(out, a, b, op))

            def exp(dst, src, k, r, p):
                ts(src, src, 87.0, ALU.min, -87.0, ALU.max)
                ts(k, src, LOG2E, ALU.mult, MAGIC, ALU.add)
                ts(k, k, -MAGIC, ALU.add)
                ts(r, k, -LN2_HI, ALU.mult)
                tt(r, r, src, ALU.add)
                ts(p, k, -LN2_LO, ALU.mult)
                tt(r, r, p, ALU.add)
                ts(p, r, EXP_POLY[0], ALU.mult, EXP_POLY[1], ALU.add)
                for c in EXP_POLY[2:]:
                    tt(p, p, r, ALU.mult)
                    ts(p, p, c, ALU.add)
                ts(k.bitcast(I32), k, 127.0, ALU.add, float(2 ** 23), ALU.mult)
                tt(dst, p, k, ALU.mult)

            pool.wait_ge(tok_taken, 3)
            flat = ein[:, :, :].rearrange("p a b -> p (a b)")
            exp(flat, flat, tmp[0][:, 0:2 * H2], tmp[1][:, 0:2 * H2], tmp[2][:, 0:2 * H2])
            dt_, ea, ai = ein[:, 0, :], ein[:, 1, :], prm[:, 0, :]
            q3 = tmp[0].rearrange("p (j h) -> p j h", j=LOGS)
            x3 = tmp[3].rearrange("p (j h) -> p j h", j=LOGS)
            tt(q3[:, 0, :], ai, dt_, ALU.mult)
            tt(x3[:, 0, :], ea, dt_, ALU.mult)
            ts(x3[:, 0, :], x3[:, 0, :], -1.0, ALU.mult)
            for l in range(1, LOGS):
                ts(q3[:, l, :], q3[:, l - 1, :], 2.0, ALU.mult)
                ts(x3[:, l, :], x3[:, l - 1, :], 2.0, ALU.mult)
            ts(tmp[1], tmp[0], INV_2PI, ALU.mult, MAGIC, ALU.add)
            ts(tmp[1], tmp[1], -MAGIC, ALU.add)
            for part in (PI2_A, PI2_B, PI2_C):
                ts(tmp[2], tmp[1], -part, ALU.mult)
                tt(tmp[0], tmp[0], tmp[2], ALU.add)
            ts(tmp[0], tmp[0], PI_DOWN, ALU.min, -PI_DOWN, ALU.max)
            exp(tmp[5], tmp[3], tmp[1], tmp[2], tmp[4])
            tt(norm[:, :], ea, ea, ALU.mult)
            tt(tmp[1][:, 0:H2], ai, ai, ALU.mult)
            pool.tensor_tensor(norm[:, :], norm[:, :], tmp[1][:, 0:H2], ALU.add).then_inc(base_ready, 1)

            pool.wait_ge(sines, 1)
            zr, zi = (zp[:, n, :, :].rearrange("p a b -> p (a b)") for n in range(2))
            tt(tmp[4], tmp[4], tmp[4], ALU.mult)
            ts(tmp[4], tmp[4], -2.0, ALU.mult, 1.0, ALU.add)
            tt(zr, tmp[4], tmp[5], ALU.mult)
            tt(zi, tmp[3], tmp[5], ALU.mult)
            br, bi = prm[:, 1, :], prm[:, 2, :]
            er, gr, gi, t0, t1 = (tmp[0][:, n * H2:(n + 1) * H2] for n in range(5))
            fr, fi = (tmp[1][:, n * H2:(n + 1) * H2] for n in range(2))
            ts(er, zp[:, 0, 0, :], -1.0, ALU.add)
            ei = zp[:, 1, 0, :]
            tt(t0, er, ea, ALU.mult)
            tt(t1, ei, ai, ALU.mult)
            tt(fr, t1, t0, ALU.subtract)
            tt(t0, er, ai, ALU.mult)
            tt(t1, ei, ea, ALU.mult)
            tt(fi, t0, t1, ALU.add)
            pool.wait_ge(norm_ready, 1)
            tt(fr, fr, norm[:, :], ALU.mult)
            tt(fi, fi, norm[:, :], ALU.mult)
            ts(fr, fr, 2.0, ALU.mult)
            ts(fi, fi, -2.0, ALU.mult)
            tt(t0, fr, br, ALU.mult)
            tt(t1, fi, bi, ALU.mult)
            tt(gr, t0, t1, ALU.subtract)
            tt(t0, fr, bi, ALU.mult)
            tt(t1, fi, br, ALU.mult)
            tt(gi, t0, t1, ALU.add)
            cr, ci = C[:, :, 0, :], C[:, :, 1, :]
            grb, gib = (v.unsqueeze(1).to_broadcast([P, CH, H2]) for v in (gr, gi))
            a0, a1, a2, a3 = (tmp[n][:, 0:CH * H2].rearrange("p (c h) -> p c h", c=CH) for n in (2, 3, 4, 5))
            tt(a0, cr, grb, ALU.mult)
            tt(a1, ci, gib, ALU.mult)
            tt(a2, cr, gib, ALU.mult)
            tt(a3, ci, grb, ALU.mult)
            tt(cr, a0, a1, ALU.subtract)
            tt(a2, a2, a3, ALU.add)
            ts(ci, a2, -1.0, ALU.mult)
            link(pool.memset(yf, 0.0))
            link(pool.memset(U[:, :, 0, 0:1], 1.0))
            link(pool.memset(U[:, :, 1, 0:1], 0.0))
            pool.wait_ge(w2_squared, KT)

            done = count[0]
            GSTEPS = 4 + 4 * LA + 4 * (LOGS - LA) + 1

            def group(g):
                at = [0]

                def signal(ins):
                    at[0] += 1
                    ins.then_inc(pool_step, 1)

                def step(ins):
                    signal(ins)
                    pool.wait_ge(pool_step, done + GSTEPS * g + at[0])

                after(pool, kmm_done, 2 * g)
                heads = bass.ds(HG * g, HG)
                for ri in range(2):
                    signal(pool.tensor_tensor(zg[:, ri, :, :], zp[:, ri, :, heads],
                                              ones[:, 0:LOGS * HG].rearrange("p (a b) -> p a b", a=LOGS), ALU.mult))
                    signal(pool.tensor_copy(Y[:, :, ri, 0, :].rearrange("p h c -> p c h"), C[:, :, ri, heads]))
                pool.wait_ge(pool_step, done + GSTEPS * g + at[0])

                def double(t, src, dst, scratch, l, w, conj):
                    shape = [P, HG, 2, w]
                    zr_, zi_ = (zg[:, n, l, :].unsqueeze(2).unsqueeze(3).to_broadcast(shape) for n in range(2))
                    step(pool.tensor_tensor(dst, src, zr_, ALU.mult))
                    step(pool.tensor_tensor(scratch, src, zi_, ALU.mult))
                    step(pool.tensor_tensor(dst[:, :, 0, :], dst[:, :, 0, :], scratch[:, :, 1, :],
                                            ALU.add if conj else ALU.subtract))
                    step(pool.tensor_tensor(dst[:, :, 1, :], dst[:, :, 1, :], scratch[:, :, 0, :],
                                            ALU.subtract if conj else ALU.add))

                for l in range(LA):
                    w = 2 ** l
                    double(U, U[:, :, :, 0:w], U[:, :, :, w:2 * w], Ut[:, :, :, 0:w], l, w, False)
                y4 = Y[:, :, :, :, :].rearrange("p h r b c -> p h r (b c)")
                for l in range(LA, LOGS):
                    w = CH * 2 ** (l - LA)
                    double(Y, y4[:, :, :, 0:w], y4[:, :, :, w:2 * w], Ut[:, :, :, 0:w], l, w, True)
                one = ones[0:N, 0:KT * CH].unsqueeze(1).unsqueeze(2).to_broadcast([N, HG, 2, KT * CH])
                signal(pool.tensor_tensor(Yb[0:N, :, :, 0, :], y4[0:N, :, :, :], one, ALU.mult))
                pool.tensor_copy(Yb[N:P, :, :, 1, :], y4[N:P, :, :, :]).then_inc(uy_ready, 1)
                assert at[0] == GSTEPS

            group(0)
            with pool.Fori(1, GROUPS) as g:
                group(g)


_INS = ["x", "x_txt", "L0_tok_log_dt", "L0_tok_B", "L0_tok_inv_A_real", "L0_tok_A_imag", "L0_txt_char_codebook",
        "L0_attn_weight", "L0_attn_mask", "L0_ffn_base_packed", "L0_ffn_scales", "L0_ffn_w_ortho"]


def kernel(**inputs):
    import numpy as _np
    import concourse.bacc as _bacc
    from concourse import mybir as _mybir
    from concourse.bass_utils import run_bass_kernel_spmd as _run

    nc = _bacc.Bacc("TRN2", target_bir_lowering=False, num_devices=1)
    arrays, args = {}, []
    for name in _INS:
        a = _np.ascontiguousarray(inputs[name])
        arrays[f"in_{name}"] = a
        args.append(nc.dram_tensor(f"in_{name}", a.shape, _mybir.dt.from_np(a.dtype), kind="ExternalInput").ap())
    heads, times, features = inputs["x"].shape[1], inputs["x_txt"].shape[1], inputs["L0_attn_weight"].shape[0]
    shape = (inputs["x"].shape[0], heads + times, features)
    args.append(nc.dram_tensor("out", shape, _mybir.dt.float32, kind="ExternalOutput").ap())
    fusion_kernel(nc, *args)
    r = _run(nc, [arrays], core_ids=[0])
    return r.results[0]["out"]
```
